# Optimizing a Trainium2 kernel written in Bass

```python
import numpy as np
import jax
import jax.numpy as jnp

def _softmax(x, axis=-1):
    return jax.nn.softmax(x, axis=axis)

def _gelu(x):
    return jax.nn.gelu(x, approximate=True)

def _silu(x):
    return jax.nn.silu(x)

def _sigmoid(x):
    return jax.nn.sigmoid(x)

def _layernorm(x, axis=-1, eps=1e-05):
    m = jnp.mean(x, axis=axis, keepdims=True)
    v = jnp.var(x, axis=axis, keepdims=True)
    return (x - m) / jnp.sqrt(v + eps)

def _scatter_add(tgt, idx, src, axis=0):
    return tgt.at[idx].add(src)

def _segment_sum(src, seg, n):
    return jax.ops.segment_sum(src, seg, n)
kernel_name = 'mk_flamingo_gated_d1_seqx_r4_a3a7af'

def setup_inputs(seed: int=0):
    np.random.seed(seed)
    _w = jnp.asarray

    def _rec_inputs():
        import jax
        import jax.numpy as jnp
        _rk = jax.random.key(seed)
        x = 2.818e-05 + 1 * jax.random.normal(jax.random.fold_in(_rk, 1), (16, 256, 256), jnp.float32)
        _lenS = 256 - jax.random.randint(jax.random.fold_in(_rk, 7), (16,), 0, max(1, 256 // 4) + 1, jnp.int32)
        _lenS2 = 256 - jax.random.randint(jax.random.fold_in(_rk, 8), (16,), 0, max(1, 256 // 4) + 1, jnp.int32)
        _ctx_1024P = jax.random.normal(jax.random.fold_in(_rk, 11), (16, 16, 256), jnp.float32)
        _ctx_1024c = jax.random.dirichlet(jax.random.fold_in(_rk, 511), 0.3 * jnp.ones((16,), jnp.float32), (16, 256))
        _ctx_1024t = jnp.einsum('bsk,bkd->bsd', _ctx_1024c, _ctx_1024P)
        _ctx_1024t = _ctx_1024t * jax.lax.rsqrt(jnp.mean(jnp.square(_ctx_1024t)) + 1e-12) * 0.953939
        ctx_1024 = 7.22013e-05 + 1.00017 * (_ctx_1024t + 0.3 * jax.random.normal(jax.random.fold_in(_rk, 611), (16, 256, 256), jnp.float32))
        _g = jax.random.normal(jax.random.fold_in(_rk, 9001), (2, 1), jnp.float32)
        _g = jnp.sign(_g) * jnp.maximum(jnp.abs(_g), 1.0) + (_g == 0) * 1.0
        g_xattn = _g[0]
        g_ffn = _g[1]
        return (x, ctx_1024, g_xattn, g_ffn)
    x, ctx_1024, g_xattn, g_ffn = _rec_inputs()

    def _L0_xattn_setup():
        import jax, jax.numpy as jnp
        import numpy as np
        INPUT_SIZE = 256
        HIDDEN_SIZE = 256
        key = jax.random.key(seed)
        kq, kc, k1, k2, k3 = jax.random.split(key, 5)
        B, LQ, LC = (8, 256, 512)
        q = jax.random.normal(kq, (B, LQ, INPUT_SIZE), dtype=jnp.float32)
        c = jax.random.normal(kc, (B, LC, INPUT_SIZE), dtype=jnp.float32)
        s = 1.0 / np.sqrt(INPUT_SIZE)
        wq = jax.random.normal(k1, (INPUT_SIZE, HIDDEN_SIZE), dtype=jnp.float32) * s
        wk = jax.random.normal(k2, (INPUT_SIZE, HIDDEN_SIZE), dtype=jnp.float32) * s
        wv = jax.random.normal(k3, (INPUT_SIZE, HIDDEN_SIZE), dtype=jnp.float32) * s
        return {'q': q, 'c': c, 'wq': wq, 'wk': wk, 'wv': wv}
    _L0_xattn_all = _L0_xattn_setup()
    _L0_xattn_in = {k: v for k, v in _L0_xattn_all.items() if k in ('wq', 'wk', 'wv')}
    del _L0_xattn_all

    def _L0_ffn_setup():
        import jax, jax.numpy as jnp
        import numpy as np
        TOP_K = 2
        key = jax.random.key(seed)
        ks = jax.random.split(key, 5)
        B, S, D, H, E = (2, 512, 256, 704, 8)
        x = jax.random.normal(ks[0], (B, S, D), dtype=jnp.float32)
        Wg = jax.random.normal(ks[1], (E, D), dtype=jnp.float32) * 0.02
        W1 = jax.random.normal(ks[2], (E, H, D), dtype=jnp.float32) * 0.02
        W2 = jax.random.normal(ks[3], (E, H, D), dtype=jnp.float32) * 0.02
        W3 = jax.random.normal(ks[4], (E, D, H), dtype=jnp.float32) * 0.02
        return {'x': x, 'Wg': Wg, 'W1': W1, 'W2': W2, 'W3': W3}
    _L0_ffn_all = _L0_ffn_setup()
    _L0_ffn_in = {k: v for k, v in _L0_ffn_all.items() if k in ('Wg', 'W1', 'W2', 'W3')}
    del _L0_ffn_all
    return {'x': x, 'ctx_1024': ctx_1024, 'g_xattn': g_xattn, 'g_ffn': g_ffn, 'L0_xattn_wq': _L0_xattn_in['wq'], 'L0_xattn_wk': _L0_xattn_in['wk'], 'L0_xattn_wv': _L0_xattn_in['wv'], 'L0_ffn_Wg': _L0_ffn_in['Wg'], 'L0_ffn_W1': _L0_ffn_in['W1'], 'L0_ffn_W2': _L0_ffn_in['W2'], 'L0_ffn_W3': _L0_ffn_in['W3']}

def reference(x, ctx_1024, g_xattn, g_ffn, L0_xattn_wq, L0_xattn_wk, L0_xattn_wv, L0_ffn_Wg, L0_ffn_W1, L0_ffn_W2, L0_ffn_W3):
    import jax
    import jax.numpy as jnp

    def _L0_xattn_ref(q, c, wq, wk, wv):
        import jax, jax.numpy as jnp
        import numpy as np
        INPUT_SIZE = 256
        HIDDEN_SIZE = 256
        Q = jnp.einsum('bld,dh->blh', c, wq)
        K = jnp.einsum('bld,dh->blh', q, wk)
        V = jnp.einsum('bld,dh->blh', q, wv)
        attn = jnp.einsum('bch,bqh->bcq', Q, K)
        attn = jax.nn.softmax(attn, axis=2)
        out = jnp.einsum('bcq,bqh->bch', attn, V)
        return out

    def _L0_ffn_ref(x, Wg, W1, W2, W3):
        import jax, jax.numpy as jnp
        import numpy as np
        TOP_K = 2
        B, S, D = x.shape
        E = Wg.shape[0]
        xt = x.reshape(B * S, D)
        scores = xt @ Wg.T
        topk_scores, topk_idx = jax.lax.top_k(scores, TOP_K)
        gate = jax.nn.silu(jnp.einsum('td,ehd->teh', xt, W1))
        up = jnp.einsum('td,ehd->teh', xt, W2)
        y = jnp.einsum('teh,edh->ted', gate * up, W3)
        onehot = jax.nn.one_hot(topk_idx, E, dtype=x.dtype)
        w = jnp.einsum('tke,tk->te', onehot, topk_scores)
        out = jnp.einsum('te,ted->td', w, y)
        return out.reshape(B, S, D)
    x = x + jnp.tanh(g_xattn[0]) * _L0_xattn_ref(ctx_1024, _layernorm(x, axis=-1), L0_xattn_wq, L0_xattn_wk, L0_xattn_wv)
    x = x + jnp.tanh(g_ffn[0]) * _L0_ffn_ref(_layernorm(x, axis=-1), L0_ffn_Wg, L0_ffn_W1, L0_ffn_W2, L0_ffn_W3)
    return x

_drawn_inputs = setup_inputs


def setup_inputs(seed=0):
    import zlib

    import numpy as np

    out = dict(_drawn_inputs(seed))
    spreads = {}
    factors = {'L0_ffn_Wg': 5.229, 'L0_ffn_W1': 4.704, 'L0_ffn_W2': 4.632, 'L0_ffn_W3': 4.647}
    for name, (base, spread) in spreads.items():
        noise = np.random.default_rng([zlib.crc32(name.encode()), seed]).standard_normal(out[name].shape)
        drawn = base * np.exp(spread * noise) if base else spread * noise
        out[name] = jnp.asarray(drawn.astype(out[name].dtype))
    for name, factor in factors.items():
        out[name] = (out[name] * factor).astype(out[name].dtype)
    return out
```

```python
from contextlib import ExitStack

import numpy as np

import concourse.bass as bass
from concourse import mybir

ALU = mybir.AluOpType
ACT = mybir.ActivationFunctionType
F32 = mybir.dt.float32
BF16 = mybir.dt.bfloat16
I32 = mybir.dt.int32
U32 = mybir.dt.uint32
AX_X = mybir.AxisListType.X

P = 128
EPS = 1e-5
TOP_K = 2


def gated_cross_attention_and_experts(nc, x, ctxT, g_xattn, g_ffn, wqT, wkT, wv, WgT, W1T, W2T, W3T, out):
    B, S, D = x.shape
    E = WgT.shape[1]
    H = W3T.shape[0]
    T = B * S
    KD = D // P
    KT = S // P
    NT = T // P
    KH = -(-H // P)
    H_LAST = H - (KH - 1) * P
    HB = H // 2
    REGION = T + P
    MOE_TILES = (TOP_K * T + E * (P - 1)) // P
    BANK = 512
    ARENA = 6784
    assert S == KT * P and D == KD * P and KT == 2 and KD == 2 and E == 8 and HB <= BANK and B % 2 == 0
    assert E * 2 == B

    x_v = x.rearrange("b (t p) d -> b p t d", p=P)
    ctx_v = ctxT.rearrange("b (c p) s -> b p c s", p=P)
    out_v = out.rearrange("b (t p) d -> (b t) p d", p=P)
    W1_v = W1T.rearrange("(c p) (e h) -> p c e h", p=P, e=E)
    W2_v = W2T.rearrange("(c p) (e h) -> p c e h", p=P, e=E)
    W3_v = W3T[0:(KH - 1) * P].rearrange("(k p) e d -> p k e d", p=P)

    xs = nc.dram_tensor("rows_by_expert", (E * REGION, D), F32, kind="Internal").ap()
    ys = nc.dram_tensor("rows_of_results", (MOE_TILES * P, D), F32, kind="Internal").ap()

    with ExitStack() as ctx:
        def sb(name, shape, dt=F32):
            return ctx.enter_context(nc.sbuf_tensor(name, shape, dt))

        def sem(name):
            return ctx.enter_context(nc.semaphore(name))

        bank = [ctx.enter_context(nc.psum_tensor(f"bank{i}", [P, BANK], F32)) for i in range(8)]
        arena = ctx.enter_context(nc.sbuf_tensor("arena", [P, ARENA], F32))

        def carve(at, shape, rows=P):
            n = int(np.prod(shape))
            assert at + n <= ARENA
            names = " ".join("abcd"[:len(shape)])
            flat = arena[0:rows, at:at + n]
            if len(shape) == 1:
                return flat
            return flat.rearrange(f"p ({names}) -> p {names}", **dict(zip("abcd", shape)))

        w1 = sb("w1", [P, KD, E * H])
        w2 = sb("w2", [P, KD, E * H])
        w3 = sb("w3", [P, KH, E * D])
        wq_t = carve(5120, [KD, D])
        wk_t = carve(5632, [KD, D])
        wv_s = sb("wv_s", [P, KD, D])
        wg_s = sb("wg_s", [P, KD, E])
        qk = sb("qk", [P, KD, D])
        ident = sb("ident", [P, P])
        before = sb("before", [P, P], BF16)
        ones = sb("ones", [P, P], BF16)
        neg_half = sb("neg_half", [P, 4])
        iota_e = sb("iota_e", [P, E])
        region_of = sb("region_of", [P, E])
        iota_p = sb("iota_p", [P, 1])
        iota_i = sb("iota_i", [1, MOE_TILES])
        upto = sb("upto", [P, E, E])
        zrow = sb("zrow", [P, D])
        gates = sb("gates", [P, 2])
        tanh_g = sb("tanh_g", [P, 2])
        xa = sb("xa", [P, NT, D])
        chosen = sb("chosen", [P, NT * TOP_K, E])
        weight = sb("weight", [P, NT, TOP_K])
        slot_f = sb("slot_f", [P, NT * TOP_K])
        ctx_s = carve(1024, [2, KD, S])
        stats = sb("stats", [P, 2, 4, 6])
        mv = sb("mv", [P, 2, 4, 2])
        var_eps = sb("var_eps", [P, 2, 4])
        rstd = sb("rstd", [P, 2, 4])
        xn1 = carve(2048, [2, KT, D])
        xn1_t = carve(3072, [KD, S])
        z_s = carve(3584, [KD, S])
        v_s = carve(4096, [2, KT, D])
        nmax = sb("nmax", [P, 2, KT])
        probs = carve(5120, [KT, S])
        sums = sb("sums", [P, 2, KT])
        rsum = sb("rsum", [P, KT])
        oscale = sb("oscale", [P, KT])
        probs_t = carve(5632, [KT, S])
        xn2 = carve(0, [2, KT, D])
        xn2_t = carve(6144, [KD, S])
        rscore = sb("rscore", [P, KT, E])
        top8 = sb("top8", [P, KT, 8])
        idx8 = sb("idx8", [P, KT, 8], U32)
        idx_f = sb("idx_f", [P, KT, TOP_K])
        mask = sb("mask", [P, KT, E], BF16)
        seen = sb("seen", [P, 2, 2, E], BF16)
        place = sb("place", [P, KT, E])
        placed = sb("placed", [P, KT, TOP_K, E])
        slot_w = sb("slot_w", [P, 2, KT * TOP_K])
        slot_i = sb("slot_i", [P, 2, KT * TOP_K], I32)
        cnt = sb("cnt", [P, E])
        cnt_i = sb("cnt_i", [P, E], I32)
        full_i = sb("full_i", [P, E], I32)
        ntile = sb("ntile", [P, E])
        ntile_upto = sb("ntile_upto", [P, E, E])
        tile_end = sb("tile_end", [P, E])
        pad_i = sb("pad_i", [1, E], I32)
        last_tile = sb("last_tile", [1, 1])
        tile_no = sb("tile_no", [1, MOE_TILES])
        is_past = carve(4224, [MOE_TILES, E], rows=1)
        past_n = carve(4792, [MOE_TILES, E], rows=1)
        tile_e = sb("tile_e", [1, MOE_TILES])
        tile_b = sb("tile_b", [1, MOE_TILES])
        tile_off = sb("tile_off", [1, MOE_TILES])
        tile_row = sb("tile_row", [1, MOE_TILES])
        e_i = sb("e_i", [1, MOE_TILES], I32)
        row_i = sb("row_i", [1, MOE_TILES], I32)
        shift_e = sb("shift_e", [P, E])
        shift_a = sb("shift_a", [P, E])
        shifted = carve(3712, [NT * TOP_K, E])
        shift = sb("shift", [P, NT * TOP_K])
        pos_i = sb("pos_i", [P, NT * TOP_K], I32)
        xg = carve(0, [2, D])
        xg_t = carve(1024, [2, KD, P])
        act_g = carve(1536, [H])
        hid = carve(2240, [H])
        hid_t = carve(2944, [KH, P])
        y_s = carve(512, [2, D])
        wsc = sb("wsc", [P, NT, TOP_K])
        NG = 4
        pos_b = sb("pos_b", [P, NG, TOP_K], I32)
        yg = carve(3712, [NG, TOP_K, D])
        acc = carve(5760, [NG, D])

        s_const = sem("s_const")
        s_w = sem("s_w")
        s_gate = sem("s_gate")
        s_tanh = sem("s_tanh")
        s_qk = sem("s_qk")
        s_qk_copied = sem("s_qk_copied")
        s_moe_w = sem("s_moe_w")
        s_x = [sem(f"s_x{k}") for k in range(2)]
        s_ctx = [sem(f"s_ctx{k}") for k in range(2)]
        s_st1 = sem("s_st1")
        s_st2 = sem("s_st2")
        s_mv = sem("s_mv")
        s_ve = sem("s_ve")
        s_rstd = sem("s_rstd")
        s_xn1 = sem("s_xn1")
        s_xn2 = sem("s_xn2")
        s_t1 = sem("s_t1")
        s_t1_copied = sem("s_t1_copied")
        s_z = sem("s_z")
        s_z_copied = sem("s_z_copied")
        s_v = sem("s_v")
        s_v_copied = sem("s_v_copied")
        s_sc = sem("s_sc")
        s_max = sem("s_max")
        s_exp = sem("s_exp")
        s_pt = sem("s_pt")
        s_pt_copied = sem("s_pt_copied")
        s_rsum = sem("s_rsum")
        s_oscale = sem("s_oscale")
        s_pv = sem("s_pv")
        s_x2 = sem("s_x2")
        s_t2 = sem("s_t2")
        s_t2_copied = sem("s_t2_copied")
        s_rt = sem("s_rt")
        s_rcopy = sem("s_rcopy")
        s_top = sem("s_top")
        s_idx = sem("s_idx")
        s_idxf = sem("s_idxf")
        s_hot = sem("s_hot")
        s_mask = sem("s_mask")
        s_seen1 = sem("s_seen1")
        s_seen = sem("s_seen")
        s_rank = sem("s_rank")
        s_place = sem("s_place")
        s_placed = sem("s_placed")
        s_slotf = sem("s_slotf")
        s_slot = sem("s_slot")
        s_scat = [sem(f"s_scat{k}") for k in range(2)]
        s_cnt = sem("s_cnt")
        s_plan = sem("s_plan")
        s_pad_at = sem("s_pad_at")
        s_map = sem("s_map")
        s_pad = sem("s_pad")
        s_xg = [sem(f"s_xg{k}") for k in range(2)]
        s_xgt = sem("s_xgt")
        s_xgt_copied = sem("s_xgt_copied")
        s_g = sem("s_g")
        s_u = sem("s_u")
        s_silu = sem("s_silu")
        s_h = sem("s_h")
        s_ht = sem("s_ht")
        s_ht_a = sem("s_ht_a")
        s_ht_b = sem("s_ht_b")
        s_y = sem("s_y")
        s_y_copied = sem("s_y_copied")
        s_ys = [sem(f"s_ys{k}") for k in range(2)]
        s_wsc = sem("s_wsc")
        s_posb = sem("s_posb")
        s_yg = [sem(f"s_yg{k}") for k in range(NG)]
        s_acc = sem("s_acc")
        s_res = sem("s_res")
        s_out = [sem(f"s_out{k}") for k in range(NG)]

        t1_ps = bank[0].rearrange("p (c s) -> p c s", c=KD)
        z_ps = bank[1].rearrange("p (c s) -> p c s", c=KD)
        v_ps = bank[2].rearrange("p (t d) -> p t d", t=KT)
        sc_ps = bank[3].rearrange("p (t s) -> p t s", t=KT)
        pt_ps = bank[4].rearrange("p (t s) -> p t s", t=KT)
        o_ps = bank[5].rearrange("p (t d) -> p t d", t=KT)
        t2_ps = bank[6].rearrange("p (c s) -> p c s", c=KD)
        rt_ps = bank[7][:, 0:KT * E]
        rank_ps = bank[7][:, 64:64 + KT * E]
        cnt_ps = bank[7][:, 128:128 + E]

        def at_least(eng, s, v):
            if not (isinstance(v, int) and v <= 0):
                eng.wait_ge(s, v)

        def wait_alone(eng, s, v):
            if not (isinstance(v, int) and v <= 0):
                if not isinstance(v, int):
                    v = eng.to_reg(v)
                eng.wait_ge(s_const, 9)
                eng.wait_ge(s, v)

        def over_batches(eng, step):
            def peeled(n):
                step(n, n // 2, n % 2, lambda m: 0 <= m < B)
            for n in range(-2, 4):
                peeled(n)
            with eng.Fori(2, B // 2 - 1) as i:
                for k in range(2):
                    step(2 * i + k, i, k, lambda m: True)
            for n in range(B - 2, B + 2):
                peeled(n)

        def over_moe_tiles(eng, step):
            def peeled(i):
                step(i, i // 2, i % 2, lambda m: 0 <= m < MOE_TILES)
            first, last = 4, MOE_TILES - 2 - MOE_TILES % 2
            for i in range(-1, first):
                peeled(i)
            with eng.Fori(first // 2, last // 2) as j:
                for k in range(2):
                    step(2 * j + k, j, k, lambda m: True)
            for i in range(last, MOE_TILES + 1):
                peeled(i)

        block = ctx.enter_context(nc.Block())

        @block.sync
        def _(sp):
            def load_x(m, j, k):
                at_least(sp, s_st1, m - 1)
                row = x_v[bass.ds(m, 1)].rearrange("a p t d -> (a p) t d")
                sp.dma_start(xa[:, bass.ds(KT * m, KT), :], row).then_inc(s_x[k], 16)

            def load_ctx(m, j, k):
                at_least(sp, s_v, m - 1)
                row = ctx_v[bass.ds(m, 1)].rearrange("a p c s -> (a p) c s")
                sp.dma_start(ctx_s[:, k], row).then_inc(s_ctx[k], 16)

            load_x(0, 0, 0)
            sp.dma_start(wq_t, wqT.rearrange("(c p) d -> p c d", p=P)).then_inc(s_w, 16)
            sp.dma_start(wk_t, wkT.rearrange("(c p) d -> p c d", p=P)).then_inc(s_w, 16)
            load_x(1, 0, 1)
            sp.dma_start(wv_s[:], wv.rearrange("(c p) d -> p c d", p=P)).then_inc(s_w, 16)
            sp.dma_start(wg_s[:], WgT.rearrange("(c p) e -> p c e", p=P)).then_inc(s_w, 16)
            with nc.allow_non_contiguous_dma(reason="one gate to every partition"):
                sp.dma_start(gates[:, 0:1], g_xattn.rearrange("(a n) -> a n", a=1).to_broadcast([P, 1])).then_inc(s_gate, 16)
                sp.dma_start(gates[:, 1:2], g_ffn.rearrange("(a n) -> a n", a=1).to_broadcast([P, 1])).then_inc(s_gate, 16)

            def step(e, k, more):
                m = 2 * e + k
                if more:
                    load_x(m + 2, e + 1, k)
                load_ctx(m, e, k)
                if k == 0:
                    sp.dma_start(w1[:, :, bass.ds(e * H, H)], W1_v[:, :, bass.ds(e, 1), :].rearrange("p c e h -> p c (e h)")).then_inc(s_moe_w, 16)
                    sp.dma_start(w3[:, 0:KH - 1, bass.ds(e * D, D)], W3_v[:, :, bass.ds(e, 1), :].rearrange("p k e d -> p k (e d)")).then_inc(s_moe_w, 16)
                else:
                    sp.dma_start(w2[:, :, bass.ds(e * H, H)], W2_v[:, :, bass.ds(e, 1), :].rearrange("p c e h -> p c (e h)")).then_inc(s_moe_w, 16)
                    sp.dma_start(w3[0:H_LAST, KH - 1, bass.ds(e * D, D)],
                                 W3T[(KH - 1) * P:H, bass.ds(e, 1), :].rearrange("p e d -> p (e d)")).then_inc(s_moe_w, 16)
            for k in range(2):
                step(0, k, True)
            with sp.Fori(1, E - 1) as e:
                for k in range(2):
                    step(e, k, True)
            for k in range(2):
                step(E - 1, k, False)

            sp.wait_ge(s_const, 9)
            sp.wait_ge(s_pad_at, 1)
            for e in range(E):
                at = sp.value_load(pad_i[0:1, e:e + 1], min_val=e * REGION, max_val=e * REGION + T)
                sp.dma_start(xs[bass.ds(at, P), :], zrow[:]).then_inc(s_pad, 16)
            for k in range(2):
                sp.wait_ge(s_scat[k], 16 * KT * TOP_K * (B // 2))
            sp.wait_ge(s_pad, 16 * E)
            sp.wait_ge(s_map, 1)

            def load_rows(i, k):
                at_least(sp, s_xgt, i - 1)
                at = sp.value_load(row_i[0:1, bass.ds(i, 1)], min_val=0, max_val=E * REGION - P)
                sp.dma_start(xg[:, k, :], xs[bass.ds(at, P), :]).then_inc(s_xg[k], 16)

            def moe_step(i, j, k, on):
                if on(i + 2):
                    load_rows(i + 2, k)
                if on(i - 1):
                    sp.wait_ge(s_y_copied, i)
                    sp.dma_start(ys[bass.ds((i - 1) * P, P), :], y_s[:, 1 - k, :]).then_inc(s_ys[1 - k], 16)
            load_rows(0, 0)
            over_moe_tiles(sp, moe_step)

            def store(t, k):
                sp.wait_ge(s_res, t + 1)
                sp.dma_start(out_v[bass.ds(t, 1)].rearrange("a p d -> (a p) d"), acc[:, k, :]).then_inc(s_out[k], 16)
            with sp.Fori(0, NT // NG) as i:
                for k in range(NG):
                    store(NG * i + k, k)
            for k in range(NG):
                sp.wait_ge(s_out[k], 16 * (NT // NG))

        @block.gpsimd
        def _(pool):
            pool.memset(ident[:], 0.0).then_inc(s_const, 1)
            pool.memset(ones[:], 1.0).then_inc(s_const, 1)
            pool.wait_ge(s_const, 2)
            pool.affine_select(out=ident[:], in_=ident[:], compare_op=ALU.not_equal, fill=1.0, base=0,
                               pattern=[[-1, P]], channel_multiplier=1).then_inc(s_const, 1)
            pool.affine_select(out=before[:], in_=ones[:], compare_op=ALU.is_gt, fill=0.0, base=0,
                               pattern=[[1, P]], channel_multiplier=-1).then_inc(s_const, 1)
            pool.memset(neg_half[:], -0.5).then_inc(s_const, 1)
            pool.memset(upto[:], 1.0).then_inc(s_const, 1)
            pool.memset(zrow[:], 0.0).then_inc(s_const, 1)
            pool.wait_ge(s_const, 7)
            pool.affine_select(out=upto[:], in_=upto[:], compare_op=ALU.is_ge, fill=0.0, base=0,
                               pattern=[[1, E], [-1, E]], channel_multiplier=0).then_inc(s_const, 1)
            pool.iota(iota_e[:], [[1, E]], base=0, channel_multiplier=0, allow_small_or_imprecise_dtypes=True)
            pool.iota(region_of[:], [[REGION, E]], base=0, channel_multiplier=0, allow_small_or_imprecise_dtypes=True)
            pool.iota(iota_i[:], [[1, MOE_TILES]], base=0, channel_multiplier=0, allow_small_or_imprecise_dtypes=True)
            pool.memset(seen[:], 0.0).then_inc(s_const, 1)

            def step(n, i, k, on):
                a, b = (0 if on(n - 1) else 2), (4 if on(n + 2) else 2)
                if on(n - 1) or on(n + 2):
                    wait_alone(pool, s_mv, n + 3)
                    pool.tensor_scalar(var_eps[:, k, a:b], mv[:, k, a:b, 1], EPS, None, ALU.add).then_inc(s_ve, 1)
                    pool.wait_ge(s_ve, n + 3)
                    pool.tensor_tensor(rstd[:, k, a:b], var_eps[:, k, a:b], neg_half[:, a:b], ALU.pow).then_inc(s_rstd, 1)
                if on(n - 2):
                    wait_alone(pool, s_slot, n - 1)
                    for t in range(KT):
                        for c in range(TOP_K):
                            col = t * TOP_K + c
                            pool.indirect_dma_start(
                                out=xs[:, :], out_offset=bass.IndirectOffsetOnAxis(ap=slot_i[:, k, col:col + 1], axis=0),
                                in_=xn2[:, k, t, :], in_offset=None).then_inc(s_scat[k], 16)
            over_batches(pool, step)

            def gather(t, k, i):
                wait_alone(pool, s_posb, t + 1)
                for c in range(TOP_K):
                    pool.indirect_dma_start(
                        out=yg[:, k, c, :], out_offset=None, in_=ys[:, :],
                        in_offset=bass.IndirectOffsetOnAxis(ap=pos_b[:, k, c:c + 1], axis=0)).then_inc(s_yg[k], 16)
            for k in range(2):
                pool.wait_ge(s_ys[k], 16 * ((MOE_TILES + 1 - k) // 2))
            with pool.Fori(0, NT // NG) as i:
                for k in range(NG):
                    gather(NG * i + k, k, i)

        @block.scalar
        def _(act):
            act.wait_ge(s_gate, 32)
            act.activation(tanh_g[:], gates[:], ACT.Tanh).then_inc(s_tanh, 1)
            act.wait_ge(s_qk, 1)
            act.activation(qk[:], z_ps, ACT.Copy).then_inc(s_qk_copied, 1)

            def step(n, i, k, on):
                if on(n):
                    act.wait_ge(s_z, n + 1)
                    act.activation(z_s, z_ps, ACT.Copy).then_inc(s_z_copied, 1)
                    act.wait_ge(s_v, n + 1)
                    act.activation(v_s[:, k], v_ps, ACT.Copy).then_inc(s_v_copied, 1)
                if on(n - 1):
                    act.wait_ge(s_pt, n)
                    act.activation(probs_t, pt_ps, ACT.Copy).then_inc(s_pt_copied, 1)
                if on(n - 2):
                    act.wait_ge(s_t2, n - 1)
                    act.activation(xn2_t, t2_ps, ACT.Copy).then_inc(s_t2_copied, 1)
                if on(n):
                    act.wait_ge(s_max, n + 1)
                    for t in range(KT):
                        ins = act.activation(probs[:, t, :], sc_ps[:, t, :], ACT.Exp, bias=nmax[:, k, t:t + 1],
                                             accum_out=sums[:, k, t:t + 1])
                    ins.then_inc(s_exp, 1)
                if on(n + 1):
                    act.wait_ge(s_t1, n + 2)
                    act.activation(xn1_t, t1_ps, ACT.Copy).then_inc(s_t1_copied, 1)
            over_batches(act, step)

            g_ps = [bank[0], bank[1]]
            def moe_step(i, j, k, on):
                if on(i):
                    act.wait_ge(s_g, i + 1)
                    at_least(act, s_h, i)
                    for b in range(2):
                        ins = act.activation(act_g[:, b * HB:(b + 1) * HB], g_ps[b][:, 0:HB], ACT.Silu)
                    ins.then_inc(s_silu, 1)
                if on(i - 1):
                    act.wait_ge(s_ht, i)
                    act.activation(hid_t[:, 0:4, :], bank[4].rearrange("p (c s) -> p c s", c=4), ACT.Copy).then_inc(s_ht_a, 1)
                if on(i + 1):
                    act.wait_ge(s_xgt, i + 2)
                    act.activation(xg_t[:, 1 - k], bank[6][:, 0:KD * P].rearrange("p (c s) -> p c s", c=KD),
                                   ACT.Copy).then_inc(s_xgt_copied, 1)
                if on(i - 1):
                    act.wait_ge(s_y, i)
                    if not (isinstance(i, int) and i < 3):
                        act.wait_ge(s_ys[1 - k], 16 * (j if k == 0 else j) - (0 if k == 1 else 16))
                    act.activation(y_s[:, 1 - k, :], bank[7][:, 0:D], ACT.Copy).then_inc(s_y_copied, 1)
            over_moe_tiles(act, moe_step)

        @block.tensor
        def _(pe):
            pe.wait_ge(s_w, 64)
            for i in range(KD):
                for h in range(KD):
                    ins = pe.matmul(z_ps[:, i, :], wk_t[:, h, i * P:(i + 1) * P], wq_t[:, h, :],
                                    start=(h == 0), stop=(h == KD - 1))
            ins.then_inc(s_qk, 1)
            pe.wait_ge(s_qk_copied, 1)
            pe.wait_ge(s_const, 9)

            def turn(dst, src, rows, cols):
                for c in range(cols):
                    for t in range(rows):
                        ins = pe.transpose(dst[:, c, t * P:(t + 1) * P], src[:, t, c * P:(c + 1) * P], ident[:])
                return ins

            def product(dst, left, right):
                for t in range(2):
                    for c in range(2):
                        ins = pe.matmul(dst[:, t, :], left[:, c, t * P:(t + 1) * P], right[:, c, :],
                                        start=(c == 0), stop=(c == 1))
                return ins

            def step(n, i, k, on):
                if on(n):
                    pe.wait_ge(s_ctx[k], 16 * i + 16)
                    at_least(pe, s_z_copied, n)
                    product(z_ps, qk, ctx_s[:, k]).then_inc(s_z, 1)
                    at_least(pe, s_v_copied, n)
                    product(v_ps, ctx_s[:, k], wv_s).then_inc(s_v, 1)
                if on(n - 1):
                    pe.wait_ge(s_exp, n)
                    at_least(pe, s_pt_copied, n - 1)
                    turn(pt_ps, probs, KT, KT).then_inc(s_pt, 1)
                if on(n - 2):
                    pe.wait_ge(s_xn2, n - 1)
                    at_least(pe, s_t2_copied, n - 2)
                    turn(t2_ps, xn2[:, k], KT, KD).then_inc(s_t2, 1)
                if on(n):
                    pe.wait_ge(s_z_copied, n + 1)
                    pe.wait_ge(s_t1_copied, n + 1)
                    product(sc_ps, xn1_t, z_s).then_inc(s_sc, 1)
                if on(n - 2):
                    pe.wait_ge(s_t2_copied, n - 1)
                    at_least(pe, s_place, n - 2)
                    for t in range(KT):
                        for c in range(KD):
                            ins = pe.matmul(rt_ps[:, t * E:(t + 1) * E], xn2_t[:, c, t * P:(t + 1) * P], wg_s[:, c, :],
                                            start=(c == 0), stop=(c == KD - 1))
                    ins.then_inc(s_rt, 1)
                if on(n - 1):
                    pe.wait_ge(s_pt_copied, n)
                    pe.wait_ge(s_v_copied, n)
                    at_least(pe, s_x2, n - 1)
                    product(o_ps, probs_t, v_s[:, 1 - k]).then_inc(s_pv, 1)
                if on(n - 2):
                    pe.wait_ge(s_seen1, n - 1)
                    pe.matmul(rank_ps, before[:], mask[:].rearrange("p t e -> p (t e)"), start=True, stop=False)
                    pe.matmul(rank_ps, ones[:], seen[:, k].rearrange("p t e -> p (t e)"),
                              start=False, stop=True).then_inc(s_rank, 1)
                if on(n + 1):
                    pe.wait_ge(s_xn1, n + 2)
                    at_least(pe, s_t1_copied, n + 1)
                    turn(t1_ps, xn1[:, 1 - k], KT, KD).then_inc(s_t1, 1)
            over_batches(pe, step)

            pe.wait_ge(s_seen, B)
            pe.wait_ge(s_place, B)
            pe.matmul(cnt_ps, ones[:], seen[:, 0, 0, :], start=True, stop=True).then_inc(s_cnt, 1)

            pe.wait_ge(s_moe_w, 16 * 4 * E)
            pe.wait_ge(s_map, 1)

            def moe_step(i, j, k, on):
                if on(i):
                    e = pe.value_load(e_i[0:1, bass.ds(i, 1)], min_val=0, max_val=E - 1)
                    pe.wait_ge(s_xgt_copied, i + 1)
                    at_least(pe, s_silu, i)
                    for b in range(2):
                        for c in range(KD):
                            ins = pe.matmul(bank[b][:, 0:HB], xg_t[:, k, c, :], w1[:, c, bass.ds(e * H + b * HB, HB)],
                                            start=(c == 0), stop=(c == KD - 1))
                    ins.then_inc(s_g, 1)
                if on(i - 1):
                    pe.wait_ge(s_h, i)
                    at_least(pe, s_ht_a, i - 1)
                    at_least(pe, s_ht_b, i - 1)
                    for c in range(KH):
                        w = P if c < KH - 1 else H_LAST
                        dst = bank[4 + c // 4][0:w, (c % 4) * P:(c % 4 + 1) * P]
                        ins = pe.transpose(dst, hid[:, c * P:c * P + w], ident[:])
                    ins.then_inc(s_ht, 1)
                if on(i):
                    for b in range(2):
                        for c in range(KD):
                            ins = pe.matmul(bank[2 + b][:, 0:HB], xg_t[:, k, c, :], w2[:, c, bass.ds(e * H + b * HB, HB)],
                                            start=(c == 0), stop=(c == KD - 1))
                    ins.then_inc(s_u, 1)
                if on(i + 1):
                    pe.wait_ge(s_xg[1 - k], 16 * (j + k) + 16)
                    at_least(pe, s_xgt_copied, i + 1)
                    for c in range(KD):
                        ins = pe.transpose(bank[6][:, c * P:(c + 1) * P], xg[:, 1 - k, c * P:(c + 1) * P], ident[:])
                    ins.then_inc(s_xgt, 1)
                if on(i - 1):
                    e1 = pe.value_load(e_i[0:1, bass.ds(i - 1, 1)], min_val=0, max_val=E - 1)
                    pe.wait_ge(s_ht_a, i)
                    pe.wait_ge(s_ht_b, i)
                    at_least(pe, s_y_copied, i - 1)
                    for c in range(KH):
                        w = P if c < KH - 1 else H_LAST
                        ins = pe.matmul(bank[7][:, 0:D], hid_t[0:w, c, :], w3[0:w, c, bass.ds(e1 * D, D)],
                                        start=(c == 0), stop=(c == KH - 1))
                    ins.then_inc(s_y, 1)
            over_moe_tiles(pe, moe_step)

        @block.vector
        def _(dve):
            dve.wait_ge(s_const, 9)
            dve.wait_ge(s_tanh, 1)

            def step(n, i, k, on):
                if on(n + 2):
                    m = n + 2
                    wait_alone(dve, s_x[k], 16 * (i + 1) + 16)
                    for t in range(KT):
                        ins = dve.bn_stats(stats[:, k, 2 + t, :], xa[:, bass.ds(KT * m + t, 1), :].rearrange("p a d -> p (a d)"))
                    ins.then_inc(s_st1, 1)
                    wait_alone(dve, s_st1, m + 1)
                    for t in range(KT):
                        ins = dve.bn_aggr(mv[:, k, 2 + t, :], stats[:, k, 2 + t, :])
                    if not on(n - 1):
                        ins.then_inc(s_mv, 1)
                if on(n - 1):
                    dve.wait_ge(s_exp, n)
                    dve.reciprocal(rsum[:], sums[:, 1 - k, :]).then_inc(s_rsum, 1)
                    dve.wait_ge(s_rsum, n)
                    dve.tensor_scalar(oscale[:], rsum[:], tanh_g[:, 0:1], None, ALU.mult).then_inc(s_oscale, 1)
                if on(n):
                    dve.wait_ge(s_sc, n + 1)
                    dve.tensor_reduce(nmax[:, k, :], sc_ps, AX_X, ALU.max, negate=True).then_inc(s_max, 1)
                if on(n - 2):
                    m = n - 2
                    hot = chosen[:, bass.ds(KT * TOP_K * m, KT * TOP_K), :]
                    dve.wait_ge(s_rt, m + 1)
                    dve.tensor_copy(rscore[:].rearrange("p t e -> p (t e)"), rt_ps).then_inc(s_rcopy, 1)
                    wait_alone(dve, s_rcopy, m + 1)
                    for t in range(KT):
                        ins = dve.max(top8[:, t, :], rscore[:, t, :])
                    ins.then_inc(s_top, 1)
                    wait_alone(dve, s_top, m + 1)
                    for t in range(KT):
                        ins = dve.max_index(idx8[:, t, :], top8[:, t, :], rscore[:, t, :])
                    ins.then_inc(s_idx, 1)
                    dve.tensor_copy(weight[:, bass.ds(KT * m, KT), :], top8[:, :, 0:TOP_K])
                    dve.wait_ge(s_idx, m + 1)
                    dve.tensor_copy(idx_f[:], idx8[:, :, 0:TOP_K]).then_inc(s_idxf, 1)
                    dve.wait_ge(s_idxf, m + 1)
                    dve.tensor_tensor(hot, idx_f[:].rearrange("p t c -> p (t c)").unsqueeze(2).to_broadcast([P, KT * TOP_K, E]),
                                      iota_e[:].unsqueeze(1).to_broadcast([P, KT * TOP_K, E]), ALU.is_equal).then_inc(s_hot, 1)
                    dve.wait_ge(s_hot, m + 1)
                    at_least(dve, s_rank, m)
                    hot4 = hot.rearrange("p (t c) e -> p t c e", c=TOP_K)
                    dve.tensor_tensor(mask[:], hot4[:, :, 0, :], hot4[:, :, 1, :], ALU.add).then_inc(s_mask, 1)
                    dve.wait_ge(s_mask, m + 1)
                    at_least(dve, s_seen, m)
                    dve.tensor_tensor(seen[:, k, 1, :], seen[:, k, 0, :], mask[:, 0, :], ALU.add).then_inc(s_seen1, 1)
                    dve.wait_ge(s_seen1, m + 1)
                    dve.tensor_tensor(seen[:, 1 - k, 0, :], seen[:, k, 1, :], mask[:, 1, :], ALU.add).then_inc(s_seen, 1)
                if on(n - 1):
                    m = n - 1
                    dve.wait_ge(s_oscale, m + 1)
                    dve.wait_ge(s_pv, m + 1)
                    for t in range(KT):
                        row = xa[:, bass.ds(KT * m + t, 1), :].rearrange("p a d -> p (a d)")
                        ins = dve.scalar_tensor_tensor(out=row, in0=o_ps[:, t, :], scalar=oscale[:, t:t + 1], in1=row,
                                                       op0=ALU.mult, op1=ALU.add)
                    ins.then_inc(s_x2, 1)
                    wait_alone(dve, s_x2, m + 1)
                    for t in range(KT):
                        row = xa[:, bass.ds(KT * m + t, 1), :].rearrange("p a d -> p (a d)")
                        ins = dve.bn_stats(stats[:, k, t, :], row)
                    ins.then_inc(s_st2, 1)
                    wait_alone(dve, s_st2, m + 1)
                    for t in range(KT):
                        ins = dve.bn_aggr(mv[:, k, t, :], stats[:, k, t, :])
                    ins.then_inc(s_mv, 1)
                if on(n - 2):
                    m = n - 2
                    dve.wait_ge(s_rank, m + 1)
                    dve.tensor_tensor(place[:], rank_ps.rearrange("p (t e) -> p t e", t=KT),
                                      region_of[:].unsqueeze(1).to_broadcast([P, KT, E]), ALU.add).then_inc(s_place, 1)
                    dve.wait_ge(s_place, m + 1)
                    for c in range(TOP_K):
                        ins = dve.tensor_tensor(placed[:, :, c, :], hot4[:, :, c, :], place[:], ALU.mult)
                    ins.then_inc(s_placed, 1)
                    dve.wait_ge(s_placed, m + 1)
                    dve.tensor_reduce(slot_w[:, k, :], placed[:].rearrange("p t c e -> p (t c) e"), AX_X,
                                      ALU.add).then_inc(s_slotf, 1)
                    dve.wait_ge(s_slotf, m + 1)
                    if not (isinstance(m, int) and m < 2):
                        wait_alone(dve, s_scat[k], 16 * KT * TOP_K * (i - 1))
                    dve.tensor_copy(slot_i[:, k, :], slot_w[:, k, :]).then_inc(s_slot, 1)
                    dve.tensor_copy(slot_f[:, bass.ds(KT * TOP_K * m, KT * TOP_K)], slot_w[:, k, :])
                if on(n - 1) or on(n + 2):
                    dve.wait_ge(s_rstd, n + 3)
                if on(n - 1):
                    m = n - 1
                    if not (isinstance(m, int) and m < 2):
                        dve.wait_ge(s_scat[1 - k], 16 * KT * TOP_K * (i - 1 + k))
                    for t in range(KT):
                        row = xa[:, bass.ds(KT * m + t, 1), :].rearrange("p a d -> p (a d)")
                        ins = dve.tensor_scalar(xn2[:, 1 - k, t, :], row, mv[:, k, t, 0:1], rstd[:, k, t:t + 1],
                                                ALU.subtract, ALU.mult)
                    ins.then_inc(s_xn2, 1)
                if on(n + 2):
                    m = n + 2
                    at_least(dve, s_t1, m - 1)
                    for t in range(KT):
                        row = xa[:, bass.ds(KT * m + t, 1), :].rearrange("p a d -> p (a d)")
                        ins = dve.tensor_scalar(xn1[:, k, t, :], row, mv[:, k, 2 + t, 0:1], rstd[:, k, 2 + t:3 + t],
                                                ALU.subtract, ALU.mult)
                    ins.then_inc(s_xn1, 1)
            over_batches(dve, step)

            plan = [0]

            def link(ins):
                plan[0] += 1
                ins.then_inc(s_plan, 1)
                dve.wait_ge(s_plan, plan[0])
            dve.wait_ge(s_cnt, 1)
            link(dve.tensor_copy(cnt[:], cnt_ps))
            dve.tensor_tensor(pad_i[:], cnt[0:1, :], region_of[0:1, :], ALU.add).then_inc(s_pad_at, 1)
            link(dve.tensor_scalar(cnt_i[:], cnt[:], float(P - 1), None, ALU.add))
            link(dve.tensor_scalar(full_i[:], cnt_i[:], P.bit_length() - 1, None, ALU.logical_shift_right))
            link(dve.tensor_copy(ntile[:], full_i[:]))
            link(dve.tensor_tensor(ntile_upto[:], upto[:], ntile[:].unsqueeze(1).to_broadcast([P, E, E]), ALU.mult))
            link(dve.tensor_reduce(tile_end[:], ntile_upto[:], AX_X, ALU.add))
            link(dve.tensor_scalar(last_tile[:], tile_end[0:1, E - 1:E], -1.0, None, ALU.add))
            link(dve.tensor_scalar(tile_no[:], iota_i[:], last_tile[:, 0:1], None, ALU.min))
            link(dve.tensor_tensor(is_past, tile_end[0:1, :].unsqueeze(1).to_broadcast([1, MOE_TILES, E]),
                                   tile_no[:].unsqueeze(2).to_broadcast([1, MOE_TILES, E]), ALU.is_le))
            link(dve.tensor_reduce(tile_e[:], is_past, AX_X, ALU.add))
            link(dve.tensor_tensor(past_n, is_past, ntile[0:1, :].unsqueeze(1).to_broadcast([1, MOE_TILES, E]), ALU.mult))
            link(dve.tensor_reduce(tile_b[:], past_n, AX_X, ALU.add))
            link(dve.tensor_tensor(tile_off[:], tile_no[:], tile_b[:], ALU.subtract))
            link(dve.tensor_scalar(tile_row[:], tile_e[:], float(REGION // P), None, ALU.mult))
            link(dve.tensor_tensor(tile_row[:], tile_row[:], tile_off[:], ALU.add))
            link(dve.tensor_copy(e_i[:], tile_e[:]))
            dve.tensor_scalar(row_i[:], tile_row[:], float(P), None, ALU.mult).then_inc(s_map, 1)
            link(dve.tensor_tensor(shift_a[:], tile_end[:], ntile[:], ALU.subtract))
            link(dve.scalar_tensor_tensor(out=shift_e[:], in0=shift_a[:], scalar=float(P), in1=region_of[:],
                                          op0=ALU.mult, op1=ALU.subtract))
            link(dve.tensor_tensor(shifted, chosen[:], shift_e[:].unsqueeze(1).to_broadcast([P, NT * TOP_K, E]), ALU.mult))
            link(dve.tensor_reduce(shift[:], shifted, AX_X, ALU.add))
            link(dve.tensor_tensor(pos_i[:], slot_f[:], shift[:], ALU.add))
            link(dve.tensor_scalar(wsc[:].rearrange("p t c -> p (t c)"), weight[:].rearrange("p t c -> p (t c)"),
                                   tanh_g[:, 1:2], None, ALU.mult))

            def moe_step(i, j, k, on):
                if on(i - 1):
                    dve.wait_ge(s_ht, i)
                    dve.tensor_copy(hid_t[:, 4, :], bank[5][:, 0:P])
                    dve.tensor_copy(hid_t[0:H_LAST, 5, :], bank[5][0:H_LAST, P:2 * P]).then_inc(s_ht_b, 1)
                if on(i):
                    dve.wait_ge(s_silu, i + 1)
                    dve.wait_ge(s_u, i + 1)
                    for b in range(2):
                        ins = dve.tensor_tensor(hid[:, b * HB:(b + 1) * HB], bank[2 + b][:, 0:HB],
                                                act_g[:, b * HB:(b + 1) * HB], ALU.mult)
                    ins.then_inc(s_h, 1)
            over_moe_tiles(dve, moe_step)

            def position(t, k):
                dve.tensor_copy(pos_b[:, k, :], pos_i[:, bass.ds(TOP_K * t, TOP_K)]).then_inc(s_posb, 1)

            def combine(t, k, i):
                dve.wait_ge(s_yg[k], 32 * i + 32)
                at_least(dve, s_out[k], 16 * i)
                row = xa[:, bass.ds(t, 1), :].rearrange("p a d -> p (a d)")
                w = wsc[:, bass.ds(t, 1), :].rearrange("p a c -> p (a c)")
                dve.scalar_tensor_tensor(out=acc[:, k, :], in0=yg[:, k, 0, :], scalar=w[:, 0:1], in1=row,
                                         op0=ALU.mult, op1=ALU.add).then_inc(s_acc, 1)
                dve.wait_ge(s_acc, t + 1)
                dve.scalar_tensor_tensor(out=acc[:, k, :], in0=yg[:, k, 1, :], scalar=w[:, 1:2], in1=acc[:, k, :],
                                         op0=ALU.mult, op1=ALU.add).then_inc(s_res, 1)
            def combine_and_position(i):
                for k in range(NG):
                    combine(NG * i + k, k, i)
                    dve.wait_ge(s_res, NG * i + k + 1)
                    position(NG * i + k + NG, k)
            for k in range(NG):
                position(k, k)
            combine_and_position(0)
            with dve.Fori(1, NT // NG - 1) as i:
                combine_and_position(i)
            for k in range(NG):
                combine(NT - NG + k, k, NT // NG - 1)


def kernel(x, ctx_1024, g_xattn, g_ffn, L0_xattn_wq, L0_xattn_wk, L0_xattn_wv, L0_ffn_Wg, L0_ffn_W1, L0_ffn_W2, L0_ffn_W3):
    import concourse.bacc as bacc
    from concourse.bass_utils import run_bass_kernel_spmd

    e, h, d = L0_ffn_W1.shape
    laid = {
        "x": x,
        "ctxT": np.transpose(ctx_1024, (0, 2, 1)),
        "g_xattn": g_xattn,
        "g_ffn": g_ffn,
        "wqT": np.transpose(L0_xattn_wq),
        "wkT": np.transpose(L0_xattn_wk),
        "wv": L0_xattn_wv,
        "WgT": np.transpose(L0_ffn_Wg),
        "W1T": np.transpose(L0_ffn_W1, (2, 0, 1)).reshape(d, e * h),
        "W2T": np.transpose(L0_ffn_W2, (2, 0, 1)).reshape(d, e * h),
        "W3T": np.transpose(L0_ffn_W3, (2, 0, 1)),
    }
    nc = bacc.Bacc("TRN2", target_bir_lowering=False, num_devices=1, dynamic_dma_scratch_size=8192)
    arrays, args = {}, []
    for name, a in laid.items():
        a = np.ascontiguousarray(a)
        arrays[f"in_{name}"] = a
        args.append(nc.dram_tensor(f"in_{name}", a.shape, mybir.dt.from_np(a.dtype), kind="ExternalInput").ap())
    args.append(nc.dram_tensor("out_0", x.shape, F32, kind="ExternalOutput").ap())
    gated_cross_attention_and_experts(nc, *args)
    r = run_bass_kernel_spmd(nc, [arrays], core_ids=[0])
    return r.results[0]["out_0"]
```

```python
from contextlib import ExitStack

import numpy as np

import concourse.bass as bass
from concourse import mybir

ALU = mybir.AluOpType
ACT = mybir.ActivationFunctionType
F32 = mybir.dt.float32
BF16 = mybir.dt.bfloat16
F16 = mybir.dt.float16
I32 = mybir.dt.int32
U32 = mybir.dt.uint32
AX_X = mybir.AxisListType.X

P = 128
EPS = 1e-5
TOP_K = 2
ONE = 1 << 23
XN_EXP = 11


def gated_cross_attention_and_experts(nc, x, ctxT, g_xattn, g_ffn, wqT, wkT, wv, WgT, W1T, W2T, W3T, out):
    B, S, D = x.shape
    E = WgT.shape[1]
    H = W3T.shape[0]
    T = B * S
    KD = D // P
    KT = S // P
    NT = T // P
    KH, KF = 6, 4
    HL = (H - KF * P) // (KH - KF)
    HC = [P] * KF + [HL] * (KH - KF)
    HB = H // 2
    ROW = D + 16
    W_AT, ID_AT = D, D + E
    RING = 8
    REGION = T + P
    MOE_TILES = (TOP_K * T + E * (P - 1)) // P
    BANK = 512
    ARENA = 6656
    PLAN = 5120
    assert S == KT * P and D == KD * P and KT == 2 and KD == 2 and E == 8 and HB <= BANK and B % 2 == 0
    assert sum(HC) == H and KF * P <= BANK and RING % 2 == 0
    assert E * 2 == B

    PARTS = [(0, 0), (1, 0), (0, 1)]
    CONSTS = 2
    ch = [sum(HC[:c]) for c in range(KH)]
    x_v = x.rearrange("b (t p) d -> b p t d", p=P)
    ctx_v = ctxT.rearrange("b (c p) s -> b p c s", p=P)
    out_v = out[0:T].rearrange("(b t p) d -> b p t d", p=P, t=KT)
    W1_v = W1T.rearrange("(c p) (e h) -> p c e h", p=P, e=E)
    W2_v = W2T.rearrange("(c p) (e h) -> p c e h", p=P, e=E)
    W3_v = W3T[0:KF * P].rearrange("(k p) e d -> p k e d", p=P)
    W3_w = W3T[KF * P:H].rearrange("(k p) e d -> p k e d", p=HL)

    xs = nc.dram_tensor("rows_by_expert", (E * REGION, ROW), F32, kind="Internal").ap()

    with ExitStack() as ctx:
        def sb(name, shape, dt=F32):
            return ctx.enter_context(nc.sbuf_tensor(name, shape, dt))

        def sem(name):
            return ctx.enter_context(nc.semaphore(name))

        psum = ctx.enter_context(nc.psum_tensor("psum", [P, 8, BANK], F32))
        bank = [psum[:, i, :] for i in range(8)]

        arena = ctx.enter_context(nc.sbuf_tensor("arena", [P, ARENA], F32))

        def carve(at, shape, rows=P):
            n = int(np.prod(shape))
            assert at + n <= ARENA
            names = " ".join("abcd"[:len(shape)])
            flat = arena[0:rows, at:at + n]
            if len(shape) == 1:
                return flat
            return flat.rearrange(f"p ({names}) -> p {names}", **dict(zip("abcd", shape)))

        w1 = [sb(f"w1_{n}", [P, KD, E * H], F16) for n in ("hi", "lo")]
        w2 = [sb(f"w2_{n}", [P, KD, E * H], F16) for n in ("hi", "lo")]
        w3 = [sb(f"w3_{n}", [P, KH, E * D], F16) for n in ("hi", "lo")]
        wg = [sb(f"wg_{n}", [P, KD, E], F16) for n in ("hi", "lo")]
        w12_in = sb("w12_in", [P, 2, KD, H])
        w3_in = sb("w3_in", [P, KH, D])
        ssq = sb("ssq", [P, 2])
        rt_unscale = sb("rt_unscale", [P, 1], I32)
        half_exp = sb("half_exp", [P, 2], I32)
        w_scale = sb("w_scale", [P, 2], I32)
        w_unscale = sb("w_unscale", [P, 3, E], I32)
        wq_t = carve(5120, [KD, D])
        wk_t = carve(5632, [KD, D])
        wv_s = sb("wv_s", [P, KD, D])
        wg_s = sb("wg_s", [P, KD, E])
        qk = sb("qk", [P, KD, D])
        ident = sb("ident", [P, P])
        ident16 = sb("ident16", [P, P], F16)
        ones_f = sb("ones_f", [P, P])
        before = sb("before", [P, P], BF16)
        ones = sb("ones", [P, P], BF16)
        neg_half = sb("neg_half", [P, 4])
        iota_e = sb("iota_e", [P, E])
        region_of = sb("region_of", [P, E])
        token = sb("token", [P, NT], I32)
        iota_i = sb("iota_i", [P, MOE_TILES])
        upto = sb("upto", [P, E, E])
        zrow = sb("zrow", [P, ROW])
        gates = sb("gates", [P, 2])
        tanh_g = sb("tanh_g", [P, 2])
        xa = sb("xa", [P, RING * KT, D])
        xn2r = sb("xn2r", [P, 2, KT, ROW])
        xn2f = carve(0, [KT, D])
        ctx_s = carve(1024, [2, KD, S])
        stats = sb("stats", [P, 2, 4, 6])
        mv = sb("mv", [P, 2, 4, 2])
        var_eps = sb("var_eps", [P, 2, 4])
        rstd = sb("rstd", [P, 2, 4])
        xn1 = carve(2048, [2, KT, D])
        xn1_t = carve(3072, [KD, S])
        z_s = carve(3584, [KD, S])
        v_s = carve(4096, [2, KT, D])
        nmax = sb("nmax", [P, 2, KT])
        probs = carve(5120, [KT, S])
        sums = sb("sums", [P, 2, KT])
        rsum = sb("rsum", [P, KT])
        oscale = sb("oscale", [P, KT])
        probs_t = carve(5632, [KT, S])
        xn2_t = carve(6144, [512]).bitcast(F16).rearrange("p (h c s) -> p h c s", h=2, c=KD)
        rscore = sb("rscore", [P, KT, E])
        top8 = sb("top8", [P, KT, 8])
        idx8 = sb("idx8", [P, KT, 8], U32)
        idx_f = sb("idx_f", [P, KT, TOP_K])
        hot = sb("hot", [P, KT, TOP_K, E])
        mask = sb("mask", [P, KT, E], BF16)
        seen = sb("seen", [P, 2, 2, E], BF16)
        place = sb("place", [P, KT, E])
        placed = sb("placed", [P, KT, TOP_K, E])
        slot_i = sb("slot_i", [P, 2, KT * TOP_K], I32)
        cnt = sb("cnt", [P, E])
        cnt_i = sb("cnt_i", [P, E], I32)
        full_i = sb("full_i", [P, E], I32)
        ntile = sb("ntile", [P, E])
        ntile_upto = sb("ntile_upto", [P, E, E])
        tile_end = sb("tile_end", [P, E])
        pad_f = sb("pad_f", [1, E])
        pad_i = sb("pad_i", [1, E], I32)
        e_i = sb("e_i", [1, MOE_TILES], I32)
        row_i = sb("row_i", [1, MOE_TILES], I32)
        unscale_y = sb("unscale_y", [P, E])
        g_unscale = sb("g_unscale", [P, MOE_TILES])
        y_unscale = sb("y_unscale", [P, MOE_TILES, E])
        is_past = carve(PLAN, [MOE_TILES, E])
        past_n = carve(PLAN + MOE_TILES * E, [MOE_TILES, E])
        tile_e = carve(PLAN + 2 * MOE_TILES * E, [MOE_TILES])
        tile_b = carve(PLAN + (2 * E + 1) * MOE_TILES, [MOE_TILES])
        tile_off = carve(PLAN + (2 * E + 2) * MOE_TILES, [MOE_TILES])
        tile_row = carve(PLAN + (2 * E + 3) * MOE_TILES, [MOE_TILES])
        is_over = carve(PLAN + (2 * E + 4) * MOE_TILES, [MOE_TILES])
        xg = carve(0, [2, ROW])
        y_s = carve(2 * ROW, [2, D])
        at = 2 * ROW + 2 * D
        xg_t = carve(at, [2, 2 * KD * P // 2]).bitcast(F16).rearrange("p b (h c s) -> p b h c s", h=2, c=KD)
        act_g = carve(at + 2 * KD * P, [2, HB])
        hid = carve(at + 2 * KD * P + H, [2, HB])
        hid_t = [carve(at + 2 * KD * P + 2 * H + h * KH * P // 2, [KH * P // 2]).bitcast(F16).rearrange("p (c s) -> p c s", c=KH)
                 for h in range(2)]
        wsel = sb("wsel", [P, 2, E])
        wsum = sb("wsum", [P, 2])
        h_max = sb("h_max", [P, 1])
        h_cap = sb("h_cap", [P, 1])
        h_exp = sb("h_exp", [P, 1], I32)
        h_scale = sb("h_scale", [P, 1], I32)
        h_unscale = sb("h_unscale", [P, 1], I32)
        y_scale = sb("y_scale", [P, 2])
        id_s = sb("id_s", [P, 2], I32)

        s_const = sem("s_const")
        s_w = sem("s_w")
        s_gate = sem("s_gate")
        s_tanh = sem("s_tanh")
        s_qk = sem("s_qk")
        s_qk_copied = sem("s_qk_copied")
        s_w12 = [sem(f"s_w12_{k}") for k in range(2)]
        s_w3 = sem("s_w3")
        s_sq = sem("s_sq")
        s_ssq = sem("s_ssq")
        s_half = sem("s_half")
        s_scale = sem("s_scale")
        s_hi12 = sem("s_hi12")
        s_hi3 = sem("s_hi3")
        s_lo12 = sem("s_lo12")
        s_lo3 = sem("s_lo3")
        s_wg = sem("s_wg")
        s_pool = sem("s_pool")
        s_x2st = [sem(f"s_x2st{k}") for k in range(2)]
        s_xf = sem("s_xf")
        s_dummy = sem("s_dummy")
        s_x = [sem(f"s_x{k}") for k in range(2)]
        s_ctx = [sem(f"s_ctx{k}") for k in range(2)]
        s_st1 = sem("s_st1")
        s_st2 = sem("s_st2")
        s_mv = sem("s_mv")
        s_ve = sem("s_ve")
        s_rstd = sem("s_rstd")
        s_xn1 = sem("s_xn1")
        s_xn2 = sem("s_xn2")
        s_t1 = sem("s_t1")
        s_t1_copied = sem("s_t1_copied")
        s_z = sem("s_z")
        s_z_copied = sem("s_z_copied")
        s_v = sem("s_v")
        s_v_copied = sem("s_v_copied")
        s_sc = sem("s_sc")
        s_max = sem("s_max")
        s_exp = sem("s_exp")
        s_pt = sem("s_pt")
        s_pt_copied = sem("s_pt_copied")
        s_rsum = sem("s_rsum")
        s_oscale = sem("s_oscale")
        s_pv = sem("s_pv")
        s_x2 = sem("s_x2")
        s_t2 = sem("s_t2")
        s_t2_copied = sem("s_t2_copied")
        s_rt = sem("s_rt")
        s_rcopy = sem("s_rcopy")
        s_top = sem("s_top")
        s_idx = sem("s_idx")
        s_idxf = sem("s_idxf")
        s_hot = sem("s_hot")
        s_mask = sem("s_mask")
        s_seen1 = sem("s_seen1")
        s_seen = sem("s_seen")
        s_rank = sem("s_rank")
        s_place = sem("s_place")
        s_placed = sem("s_placed")
        s_slot = sem("s_slot")
        s_scat = [sem(f"s_scat{k}") for k in range(2)]
        s_cnt = sem("s_cnt")
        s_plan = sem("s_plan")
        s_pad_at = sem("s_pad_at")
        s_map = sem("s_map")
        s_pad = sem("s_pad")
        s_xg = [sem(f"s_xg{k}") for k in range(2)]
        s_xgt = sem("s_xgt")
        s_xgt_copied = sem("s_xgt_copied")
        s_g = sem("s_g")
        s_u = sem("s_u")
        s_silu = sem("s_silu")
        s_h = sem("s_h")
        s_ht = sem("s_ht")
        s_ht_a = sem("s_ht_a")
        s_ht_b = sem("s_ht_b")
        s_y = sem("s_y")
        s_y_copied = sem("s_y_copied")
        s_meta = sem("s_meta")
        s_wsel = sem("s_wsel")
        s_hmul = sem("s_hmul")
        s_hmax = sem("s_hmax")
        s_hcap = sem("s_hcap")
        s_hexp = sem("s_hexp")
        s_hscale = sem("s_hscale")
        s_yscale = sem("s_yscale")
        s_add = [sem(f"s_add{k}") for k in range(2)]

        t1_ps = bank[0].rearrange("p (c s) -> p c s", c=KD)
        z_ps = bank[1].rearrange("p (c s) -> p c s", c=KD)
        v_ps = bank[2].rearrange("p (t d) -> p t d", t=KT)
        sc_ps = bank[3].rearrange("p (t s) -> p t s", t=KT)
        pt_ps = bank[4].rearrange("p (t s) -> p t s", t=KT)
        o_ps = bank[5].rearrange("p (t d) -> p t d", t=KT)
        t2_ps = bank[6].bitcast(F16).rearrange("p (h c s) -> p h c s", h=2, c=KD)
        rt_ps = bank[7][:, 0:KT * E]
        rank_ps = bank[7][:, 64:64 + KT * E]
        cnt_ps = bank[7][:, 128:128 + E]
        ssq_ps = bank[7][:, 192:194]
        g_ps = psum[:, 0:2, 0:HB]
        u_ps = psum[:, 2:4, 0:HB]
        ht_ps = [bank[4].rearrange("p (c s) -> p c s", c=KF), bank[5][0:HL, 0:2 * P].rearrange("p (c s) -> p c s", c=2)]
        xgt_ps = bank[6][:, 0:KD * P].bitcast(F16).rearrange("p (h c s) -> p h c s", h=2, c=KD)
        y_ps = bank[7][:, 0:D]

        def at_least(eng, s, v):
            if not (isinstance(v, int) and v <= 0):
                eng.wait_ge(s, v)

        def wait_alone(eng, s, v):
            if not (isinstance(v, int) and v <= 0):
                if not isinstance(v, int):
                    v = eng.to_reg(v)
                eng.wait_ge(s_const, CONSTS)
                eng.wait_ge(s, v)

        def x_at(i, k):
            return KT * (2 * (i % (RING // 2)) + k)

        def over_batches(eng, step):
            def peeled(n):
                step(n, n // 2, n % 2, lambda m: 0 <= m < B)
            for n in range(-2, 4):
                peeled(n)
            with eng.Fori(2, B // 2 - 1) as i:
                for k in range(2):
                    step(2 * i + k, i, k, lambda m: True)
            for n in range(B - 2, B + 2):
                peeled(n)

        def over_moe_tiles(eng, step):
            def peeled(i):
                step(i, i // 2, i % 2, lambda m: 0 <= m < MOE_TILES)
            first, last = 4, MOE_TILES - 2 - MOE_TILES % 2
            for i in range(-1, first):
                peeled(i)
            with eng.Fori(first // 2, last // 2) as j:
                for k in range(2):
                    step(2 * j + k, j, k, lambda m: True)
            for i in range(last, MOE_TILES + 1):
                peeled(i)

        block = ctx.enter_context(nc.Block())

        @block.sync
        def _(sp):
            def load_x(m, i, k):
                at_least(sp, s_st1, m - 1)
                at_least(sp, s_x2st[k], 16 * (i - RING // 2 + 1))
                row = x_v[bass.ds(m, 1)].rearrange("a p t d -> (a p) t d")
                sp.dma_start(xa[:, bass.ds(x_at(i, k), KT), :], row).then_inc(s_x[k], 16)

            def load_ctx(m, k):
                at_least(sp, s_v, m - 1)
                row = ctx_v[bass.ds(m, 1)].rearrange("a p c s -> (a p) c s")
                sp.dma_start(ctx_s[:, k], row).then_inc(s_ctx[k], 16)

            def load_w12(m, e, k):
                at_least(sp, s_lo12, m - 1)
                src = (W1_v, W2_v)[k][:, :, bass.ds(e, 1), :].rearrange("p c e h -> p c (e h)")
                sp.dma_start(w12_in[:, k], src).then_inc(s_w12[k], 16)

            def load_w3(e):
                at_least(sp, s_lo3, e)
                sp.dma_start(w3_in[:, 0:KF, :], W3_v[:, :, bass.ds(e, 1), :].rearrange("p k e d -> p k (e d)")).then_inc(s_w3, 16)
                sp.dma_start(w3_in[0:HL, KF:KH, :], W3_w[:, :, bass.ds(e, 1), :].rearrange("p k e d -> p k (e d)")).then_inc(s_w3, 16)

            load_x(0, 0, 0)
            sp.dma_start(wq_t, wqT.rearrange("(c p) d -> p c d", p=P)).then_inc(s_w, 16)
            sp.dma_start(wk_t, wkT.rearrange("(c p) d -> p c d", p=P)).then_inc(s_w, 16)
            load_ctx(0, 0)
            sp.dma_start(wv_s[:], wv.rearrange("(c p) d -> p c d", p=P)).then_inc(s_w, 16)
            load_x(1, 0, 1)
            sp.dma_start(wg_s[:], WgT.rearrange("(c p) e -> p c e", p=P)).then_inc(s_w, 16)
            with nc.allow_non_contiguous_dma(reason="one gate to every partition"):
                sp.dma_start(gates[:, 0:1], g_xattn.rearrange("(a n) -> a n", a=1).to_broadcast([P, 1])).then_inc(s_gate, 16)
                sp.dma_start(gates[:, 1:2], g_ffn.rearrange("(a n) -> a n", a=1).to_broadcast([P, 1])).then_inc(s_gate, 16)
            load_w12(0, 0, 0)
            sp.wait_ge(s_const, CONSTS)
            sp.dma_start(out[T:T + P, :], zrow[:, 0:D]).then_inc(s_dummy, 16)

            def step(m, i, k, x_on=True, more=True):
                if x_on:
                    load_x(m + 2, i + 1, k)
                if more:
                    load_ctx(m + 1, 1 - k)
                    load_w12(m + 1, i + k, 1 - k)
                if k == 0:
                    load_w3(i)
            for m in range(6):
                step(m, m // 2, m % 2)
            with sp.Fori(3, E - 1) as i:
                for k in range(2):
                    step(2 * i + k, i, k)
            for k in range(2):
                step(B - 2 + k, E - 1, k, False, k == 0)

            sp.wait_ge(s_pad_at, 1)
            for e in range(E):
                at = sp.value_load(pad_i[0:1, e:e + 1], min_val=e * REGION, max_val=e * REGION + T)
                sp.dma_start(xs[bass.ds(at, P), :], zrow[:]).then_inc(s_pad, 16)
            for k in range(2):
                sp.wait_ge(s_scat[k], 16 * KT * TOP_K * (B // 2))
            sp.wait_ge(s_pad, 16 * E)
            sp.wait_ge(s_map, 1)

            def load_rows(i, k):
                at_least(sp, s_xgt, i - 1)
                at_least(sp, s_meta, i - 1)
                at = sp.value_load(row_i[0:1, bass.ds(i, 1)], min_val=0, max_val=E * REGION - P)
                sp.dma_start(xg[:, k, :], xs[bass.ds(at, P), :]).then_inc(s_xg[k], 16)

            load_rows(0, 0)
            load_rows(1, 1)
            load_rows(2, 0)
            load_rows(3, 1)
            with sp.Fori(2, MOE_TILES // 2) as j:
                for k in range(2):
                    load_rows(2 * j + k, k)
            for i in range(MOE_TILES - MOE_TILES % 2, MOE_TILES):
                load_rows(i, i % 2)
            for k in range(2):
                sp.wait_ge(s_add[k], 16 * ((MOE_TILES + 1 - k) // 2))

        @block.gpsimd
        def _(pool):
            pool.memset(ident[:], 0.0).then_inc(s_pool, 1)
            pool.memset(ones[:], 1.0).then_inc(s_pool, 1)
            pool.memset(zrow[:], 0.0).then_inc(s_pool, 1)
            pool.memset(upto[:], 1.0).then_inc(s_pool, 1)
            pool.wait_ge(s_pool, 4)
            pool.affine_select(out=ident[:], in_=ident[:], compare_op=ALU.not_equal, fill=1.0, base=0,
                               pattern=[[-1, P]], channel_multiplier=1).then_inc(s_pool, 1)
            pool.affine_select(out=before[:], in_=ones[:], compare_op=ALU.is_gt, fill=0.0, base=0,
                               pattern=[[1, P]], channel_multiplier=-1)
            pool.affine_select(out=upto[:], in_=upto[:], compare_op=ALU.is_ge, fill=0.0, base=0,
                               pattern=[[1, E], [-1, E]], channel_multiplier=0)
            pool.iota(zrow[:, ID_AT:ID_AT + 1].bitcast(I32), [[0, 1]], base=T, channel_multiplier=1)
            pool.memset(neg_half[:], -0.5)
            pool.memset(ones_f[:], 1.0)
            pool.memset(seen[:], 0.0)
            pool.memset(xn2r[:], 0.0)
            pool.memset(w3_in[:], 0.0)
            pool.wait_ge(s_pool, 5)
            pool.tensor_copy(ident16[:], ident[:])
            pool.iota(token[:], [[P, NT]], base=0, channel_multiplier=1)
            pool.iota(iota_e[:], [[1, E]], base=0, channel_multiplier=0, allow_small_or_imprecise_dtypes=True)
            pool.iota(region_of[:], [[REGION, E]], base=0, channel_multiplier=0, allow_small_or_imprecise_dtypes=True)
            pool.iota(iota_i[:], [[1, MOE_TILES]], base=0, channel_multiplier=0,
                      allow_small_or_imprecise_dtypes=True).then_inc(s_const, CONSTS)

            def step(n, i, k, on):
                a, b = (0 if on(n - 1) else 2), (4 if on(n + 2) else 2)
                if a < b:
                    wait_alone(pool, s_mv, n + 3)
                if on(n - 1):
                    ins = pool.tensor_scalar(var_eps[:, k, 0:2], mv[:, k, 0:2, 1], EPS, 2.0 ** (-2 * XN_EXP), ALU.add, ALU.mult)
                if on(n + 2):
                    ins = pool.tensor_scalar(var_eps[:, k, 2:4], mv[:, k, 2:4, 1], EPS, None, ALU.add)
                if a < b:
                    ins.then_inc(s_ve, 1)
                    pool.wait_ge(s_ve, n + 3)
                    pool.tensor_tensor(rstd[:, k, a:b], var_eps[:, k, a:b], neg_half[:, a:b], ALU.pow).then_inc(s_rstd, 1)
                if on(n - 1):
                    pool.wait_ge(s_xf, n)
                    pool.tensor_tensor(xn2r[:, 1 - k, :, D // 2:D].bitcast(F16), xn2f,
                                       xn2r[:, 1 - k, :, 0:D // 2].bitcast(F16), ALU.subtract).then_inc(s_xn2, 1)
                if on(n - 2):
                    wait_alone(pool, s_slot, n - 1)
                    for t in range(KT):
                        for c in range(TOP_K):
                            col = t * TOP_K + c
                            pool.indirect_dma_start(
                                out=xs[:, :], out_offset=bass.IndirectOffsetOnAxis(ap=slot_i[:, k, col:col + 1], axis=0),
                                in_=xn2r[:, k, t, :], in_offset=None).then_inc(s_scat[k], 16)
            over_batches(pool, step)

            for k in range(2):
                pool.wait_ge(s_x2st[k], 16 * (B // 2))
            pool.wait_ge(s_dummy, 16)

            def add_rows(i, j, k):
                if k == 0:
                    if not (isinstance(i, int) and i == 0):
                        pool.wait_ge(s_add[1], 16 * j)
                else:
                    pool.wait_ge(s_add[0], 16 * j + 16)
                wait_alone(pool, s_y_copied, i + 1)
                pool.indirect_dma_start(
                    out=out[:, :], out_offset=bass.IndirectOffsetOnAxis(ap=id_s[:, k:k + 1], axis=0),
                    in_=y_s[:, k, :], in_offset=None, compute_op=ALU.add).then_inc(s_add[k], 16)
            add_rows(0, 0, 0)
            add_rows(1, 0, 1)
            with pool.Fori(1, MOE_TILES // 2) as j:
                for k in range(2):
                    add_rows(2 * j + k, j, k)
            for i in range(MOE_TILES - MOE_TILES % 2, MOE_TILES):
                add_rows(i, i // 2, i % 2)

        @block.scalar
        def _(act):
            act.wait_ge(s_gate, 32)
            act.activation(tanh_g[:], gates[:], ACT.Tanh).then_inc(s_tanh, 1)
            act.wait_ge(s_qk, 1)
            act.activation(qk[:], z_ps, ACT.Copy).then_inc(s_qk_copied, 1)
            act.wait_ge(s_w, 64)
            act.activation(wg[0][:].bitcast(BF16), wg_s[:], ACT.Square,
                           accum_out=ssq[:, 0:1]).then_inc(s_sq, 1)
            act.wait_ge(s_scale, 1)
            act.activation(wg[0][:], wg_s[:], ACT.Copy, scale=w_scale[:, 0:1].bitcast(F32)).then_inc(s_wg, 1)

            def step(n, i, k, on):
                if on(n):
                    act.wait_ge(s_z, n + 1)
                    act.activation(z_s, z_ps, ACT.Copy).then_inc(s_z_copied, 1)
                    act.wait_ge(s_v, n + 1)
                    act.activation(v_s[:, k], v_ps, ACT.Copy).then_inc(s_v_copied, 1)
                    act.wait_ge(s_w12[k], 16 * i + 16)
                    wait_alone(act, s_ssq, n + 1)
                    ins = act.activation((w1, w2)[k][0][:, :, bass.ds(i * H, H)].bitcast(BF16), w12_in[:, k], ACT.Square,
                                         accum_out=ssq[:, 0:1])
                    if k == 1:
                        wait_alone(act, s_w3, 32 * i + 32)
                        ins = act.activation(w3[0][:, :, bass.ds(i * D, D)].bitcast(BF16), w3_in[:], ACT.Square,
                                             accum_out=ssq[:, 1:2])
                    ins.then_inc(s_sq, 1)
                if on(n - 1):
                    act.wait_ge(s_pt, n)
                    act.activation(probs_t, pt_ps, ACT.Copy).then_inc(s_pt_copied, 1)
                if on(n - 2):
                    act.wait_ge(s_t2, n - 1)
                    act.activation(xn2_t, t2_ps, ACT.Copy).then_inc(s_t2_copied, 1)
                    act.wait_ge(s_x2, n - 1)
                    at_least(act, s_x2st[k], 16 * (i - 1))
                    act.dma_start(out_v[bass.ds(n - 2, 1)].rearrange("a p t d -> (a p) t d"),
                                  xa[:, bass.ds(x_at(i - 1, k), KT), :]).then_inc(s_x2st[k], 16)
                if on(n):
                    act.wait_ge(s_max, n + 1)
                    for t in range(KT):
                        ins = act.activation(probs[:, t, :], sc_ps[:, t, :], ACT.Exp, bias=nmax[:, k, t:t + 1],
                                             accum_out=sums[:, k, t:t + 1])
                    ins.then_inc(s_exp, 1)
                if on(n + 1):
                    act.wait_ge(s_t1, n + 2)
                    act.activation(xn1_t, t1_ps, ACT.Copy).then_inc(s_t1_copied, 1)
                if on(n):
                    wait_alone(act, s_scale, n + 2)
                    act.activation((w1, w2)[k][0][:, :, bass.ds(i * H, H)], w12_in[:, k], ACT.Copy,
                                   scale=w_scale[:, 0:1].bitcast(F32)).then_inc(s_hi12, 1)
                    if k == 1:
                        act.activation(w3[0][:, :, bass.ds(i * D, D)], w3_in[:], ACT.Copy,
                                       scale=w_scale[:, 1:2].bitcast(F32)).then_inc(s_hi3, 1)
            over_batches(act, step)

            act.wait_ge(s_map, 2)

            def moe_step(i, j, k, on):
                if on(i):
                    act.wait_ge(s_g, i + 1)
                    at_least(act, s_hmul, i)
                    act.activation(act_g, g_ps, ACT.Silu, scale=g_unscale[:, bass.ds(i, 1)]).then_inc(s_silu, 1)
                if on(i - 1):
                    act.wait_ge(s_ht, i)
                    act.activation(hid_t[0][:, 0:KF, :], ht_ps[0], ACT.Copy).then_inc(s_ht_a, 1)
                    act.activation(hid_t[0][0:HL, KF:KH, :], ht_ps[1], ACT.Copy).then_inc(s_ht_a, 1)
                    act.wait_ge(s_y, i)
                    act.wait_ge(s_yscale, i)
                    if not (isinstance(i, int) and i < 3):
                        act.wait_ge(s_add[1 - k], 16 * (j - 1 + k))
                    act.activation(y_s[:, 1 - k, :], y_ps, ACT.Copy, scale=y_scale[:, 1 - k:2 - k]).then_inc(s_y_copied, 1)
            over_moe_tiles(act, moe_step)

        @block.tensor
        def _(pe):
            pe.wait_ge(s_w, 64)
            for i in range(KD):
                for h in range(KD):
                    ins = pe.matmul(z_ps[:, i, :], wk_t[:, h, i * P:(i + 1) * P], wq_t[:, h, :],
                                    start=(h == 0), stop=(h == KD - 1))
            ins.then_inc(s_qk, 1)
            pe.wait_ge(s_qk_copied, 1)
            pe.wait_ge(s_const, CONSTS)
            pe.wait_ge(s_sq, 1)
            pe.matmul(ssq_ps[:, 0:1], ones_f[:], ssq[:, 0:1], start=True, stop=True).then_inc(s_ssq, 1)

            def turn(dst, src, rows, cols, ident=ident):
                for c in range(cols):
                    for t in range(rows):
                        ins = pe.transpose(dst[:, c, t * P:(t + 1) * P], src[:, t, c * P:(c + 1) * P], ident[:])
                return ins

            def product(dst, left, right):
                for t in range(2):
                    for c in range(2):
                        ins = pe.matmul(dst[:, t, :], left[:, c, t * P:(t + 1) * P], right[:, c, :],
                                        start=(c == 0), stop=(c == 1))
                return ins

            def step(n, i, k, on):
                if on(n):
                    pe.wait_ge(s_ctx[k], 16 * i + 16)
                    at_least(pe, s_z_copied, n)
                    product(z_ps, qk, ctx_s[:, k]).then_inc(s_z, 1)
                    at_least(pe, s_v_copied, n)
                    product(v_ps, ctx_s[:, k], wv_s).then_inc(s_v, 1)
                if on(n - 1):
                    pe.wait_ge(s_exp, n)
                    at_least(pe, s_pt_copied, n - 1)
                    turn(pt_ps, probs, KT, KT).then_inc(s_pt, 1)
                if on(n - 2):
                    pe.wait_ge(s_xn2, n - 1)
                    at_least(pe, s_t2_copied, n - 2)
                    for h in range(2):
                        ins = turn(t2_ps[:, h], xn2r[:, k, :, h * D // 2:(h + 1) * D // 2].bitcast(F16), KT, KD, ident16)
                    ins.then_inc(s_t2, 1)
                if on(n):
                    pe.wait_ge(s_z_copied, n + 1)
                    pe.wait_ge(s_t1_copied, n + 1)
                    product(sc_ps, xn1_t, z_s).then_inc(s_sc, 1)
                    at_least(pe, s_place, n - 2)
                    pe.wait_ge(s_sq, n + 2)
                    w = 1 + k
                    pe.matmul(ssq_ps[:, 0:w], ones_f[:], ssq[:, 0:w], start=True, stop=True).then_inc(s_ssq, 1)
                if on(n - 2):
                    pe.wait_ge(s_t2_copied, n - 1)
                    at_least(pe, s_place, n - 2)
                    pe.wait_ge(s_wg, 2)
                    for t in range(KT):
                        for q, (a, b) in enumerate(PARTS):
                            for c in range(KD):
                                ins = pe.matmul(rt_ps[:, t * E:(t + 1) * E], xn2_t[:, a, c, t * P:(t + 1) * P], wg[b][:, c, :],
                                                start=(q == 0 and c == 0), stop=(q == 2 and c == KD - 1))
                    ins.then_inc(s_rt, 1)
                if on(n - 1):
                    pe.wait_ge(s_pt_copied, n)
                    pe.wait_ge(s_v_copied, n)
                    at_least(pe, s_x2, n - 1)
                    product(o_ps, probs_t, v_s[:, 1 - k]).then_inc(s_pv, 1)
                if on(n - 2):
                    pe.wait_ge(s_seen1, n - 1)
                    pe.matmul(rank_ps, before[:], mask[:].rearrange("p t e -> p (t e)"), start=True, stop=False)
                    pe.matmul(rank_ps, ones[:], seen[:, k].rearrange("p t e -> p (t e)"),
                              start=False, stop=True).then_inc(s_rank, 1)
                if on(n + 1):
                    pe.wait_ge(s_xn1, n + 2)
                    at_least(pe, s_t1_copied, n + 1)
                    turn(t1_ps, xn1[:, 1 - k], KT, KD).then_inc(s_t1, 1)
            over_batches(pe, step)

            pe.wait_ge(s_seen, B)
            pe.wait_ge(s_place, B)
            pe.matmul(cnt_ps, ones[:], seen[:, 0, 0, :], start=True, stop=True).then_inc(s_cnt, 1)

            pe.wait_ge(s_lo12, 2 * E)
            pe.wait_ge(s_lo3, E)
            pe.wait_ge(s_map, 1)

            def turn_rows(i, j, k):
                pe.wait_ge(s_xg[k], 16 * j + 16)
                at_least(pe, s_xgt_copied, i)
                for h in range(2):
                    for c in range(KD):
                        ins = pe.transpose(xgt_ps[:, h, c, :], xg[:, k, h * D // 2 + c * P // 2:h * D // 2 + (c + 1) * P // 2].bitcast(F16),
                                           ident16[:])
                ins.then_inc(s_xgt, 1)

            def to_hidden(ps, w, e, k):
                for b in range(2):
                    for q, (x_part, w_part) in enumerate(PARTS):
                        for c in range(KD):
                            ins = pe.matmul(ps[:, b, :], xg_t[:, k, x_part, c, :], w[w_part][:, c, bass.ds(e * H + b * HB, HB)],
                                            start=(q == 0 and c == 0), stop=(q == 2 and c == KD - 1))
                return ins

            def moe_step(i, j, k, on):
                if on(i):
                    e = pe.value_load(e_i[0:1, bass.ds(i, 1)], min_val=0, max_val=E - 1)
                    pe.wait_ge(s_xgt_copied, i + 1)
                    at_least(pe, s_silu, i)
                    to_hidden(g_ps, w1, e, k).then_inc(s_g, 1)
                if on(i - 1):
                    pe.wait_ge(s_h, i)
                    at_least(pe, s_ht_b, 2 * i - 2)
                    for c in range(KH):
                        dst = ht_ps[0][:, c, :] if c < KF else ht_ps[1][:, c - KF, :]
                        flat = hid.rearrange("p b h -> p (b h)")
                        ins = pe.transpose(dst, flat[:, ch[c]:ch[c] + HC[c]], ident[:])
                    ins.then_inc(s_ht, 1)
                if on(i + 1):
                    turn_rows(i + 1, j + k, 1 - k)
                if on(i):
                    at_least(pe, s_hmul, i)
                    to_hidden(u_ps, w2, e, k).then_inc(s_u, 1)
                if on(i - 1):
                    e1 = pe.value_load(e_i[0:1, bass.ds(i - 1, 1)], min_val=0, max_val=E - 1)
                    pe.wait_ge(s_ht_b, 2 * i)
                    at_least(pe, s_y_copied, i - 1)
                    for q, (h_part, w_part) in enumerate(PARTS):
                        for c in range(KH):
                            ins = pe.matmul(y_ps, hid_t[h_part][0:HC[c], c, :], w3[w_part][0:HC[c], c, bass.ds(e1 * D, D)],
                                            start=(q == 0 and c == 0), stop=(q == 2 and c == KH - 1))
                    ins.then_inc(s_y, 1)
            over_moe_tiles(pe, moe_step)

        @block.vector
        def _(dve):
            dve.wait_ge(s_const, CONSTS)
            dve.wait_ge(s_tanh, 1)

            def scales(w, n):
                dve.tensor_scalar(half_exp[:, 0:w], ssq_ps[:, 0:w].bitcast(I32), 24, None,
                                  ALU.logical_shift_right).then_inc(s_half, 1)
                dve.wait_ge(s_half, n + 2)
                dve.tensor_scalar(w_scale[:, 0:w], half_exp[:, 0:w], -float(ONE), 203.0 * ONE, ALU.mult,
                                  ALU.add).then_inc(s_scale, 1)

            def unscale(dst, col, less):
                return dve.tensor_scalar(dst, half_exp[:, col:col + 1], float(ONE), float((51 - less) * ONE), ALU.mult, ALU.add)

            dve.wait_ge(s_ssq, 1)
            scales(1, -1)
            unscale(rt_unscale[:], 0, XN_EXP)
            dve.wait_ge(s_scale, 1)
            dve.wait_ge(s_wg, 1)
            dve.scalar_tensor_tensor(out=wg[1][:], in0=wg_s[:], scalar=w_scale[:, 0:1].bitcast(F32), in1=wg[0][:],
                                     op0=ALU.mult, op1=ALU.subtract).then_inc(s_wg, 1)

            def step(n, i, k, on):
                if on(n + 2):
                    m = n + 2
                    at = x_at(i + 1, k)
                    wait_alone(dve, s_x[k], 16 * (i + 1) + 16)
                    for t in range(KT):
                        ins = dve.bn_stats(stats[:, k, 2 + t, :], xa[:, bass.ds(at + t, 1), :].rearrange("p a d -> p (a d)"))
                    ins.then_inc(s_st1, 1)
                    wait_alone(dve, s_st1, m + 1)
                    for t in range(KT):
                        ins = dve.bn_aggr(mv[:, k, 2 + t, :], stats[:, k, 2 + t, :])
                    if not on(n - 1):
                        ins.then_inc(s_mv, 1)
                if on(n - 1):
                    dve.wait_ge(s_exp, n)
                    dve.reciprocal(rsum[:], sums[:, 1 - k, :]).then_inc(s_rsum, 1)
                    dve.wait_ge(s_rsum, n)
                    dve.tensor_scalar(oscale[:], rsum[:], tanh_g[:, 0:1], None, ALU.mult).then_inc(s_oscale, 1)
                if on(n):
                    dve.wait_ge(s_sc, n + 1)
                    dve.tensor_reduce(nmax[:, k, :], sc_ps, AX_X, ALU.max, negate=True).then_inc(s_max, 1)
                    dve.wait_ge(s_ssq, n + 2)
                    if on(n - 2):
                        dve.wait_ge(s_rt, n - 1)
                    at_least(dve, s_hi12, n)
                    scales(1 + k, n)
                    unscale(w_unscale[:, k, bass.ds(i, 1)], 0, XN_EXP)
                    if k == 1:
                        unscale(w_unscale[:, 2, bass.ds(i, 1)], 1, 0)
                if on(n - 2):
                    m = n - 2
                    dve.wait_ge(s_rt, m + 1)
                    dve.tensor_scalar(rscore[:].rearrange("p t e -> p (t e)"), rt_ps, rt_unscale[:].bitcast(F32), None,
                                      ALU.mult).then_inc(s_rcopy, 1)
                    wait_alone(dve, s_rcopy, m + 1)
                    for t in range(KT):
                        ins = dve.max(top8[:, t, :], rscore[:, t, :])
                    ins.then_inc(s_top, 1)
                    wait_alone(dve, s_top, m + 1)
                    for t in range(KT):
                        ins = dve.max_index(idx8[:, t, :], top8[:, t, :], rscore[:, t, :])
                    ins.then_inc(s_idx, 1)
                    dve.tensor_copy(xn2r[:, k, :, ID_AT].bitcast(I32), token[:, bass.ds(KT * m, KT)])
                    dve.wait_ge(s_idx, m + 1)
                    dve.tensor_copy(idx_f[:], idx8[:, :, 0:TOP_K]).then_inc(s_idxf, 1)
                    dve.wait_ge(s_idxf, m + 1)
                    dve.tensor_tensor(hot[:].rearrange("p t c e -> p (t c) e"),
                                      idx_f[:].rearrange("p t c -> p (t c)").unsqueeze(2).to_broadcast([P, KT * TOP_K, E]),
                                      iota_e[:].unsqueeze(1).to_broadcast([P, KT * TOP_K, E]), ALU.is_equal).then_inc(s_hot, 1)
                    dve.wait_ge(s_hot, m + 1)
                    at_least(dve, s_rank, m)
                    dve.tensor_tensor(mask[:], hot[:, :, 0, :], hot[:, :, 1, :], ALU.add).then_inc(s_mask, 1)
                    dve.wait_ge(s_mask, m + 1)
                    at_least(dve, s_seen, m)
                    dve.tensor_tensor(xn2r[:, k, :, W_AT:W_AT + E], mask[:], rscore[:], ALU.mult)
                    dve.tensor_tensor(seen[:, k, 1, :], seen[:, k, 0, :], mask[:, 0, :], ALU.add).then_inc(s_seen1, 1)
                    dve.wait_ge(s_seen1, m + 1)
                    dve.tensor_tensor(seen[:, 1 - k, 0, :], seen[:, k, 1, :], mask[:, 1, :], ALU.add).then_inc(s_seen, 1)
                if on(n - 1):
                    m = n - 1
                    at = x_at(*((i - 1, 1) if k == 0 else (i, 0)))
                    dve.wait_ge(s_oscale, m + 1)
                    dve.wait_ge(s_pv, m + 1)
                    for t in range(KT):
                        row = xa[:, bass.ds(at + t, 1), :].rearrange("p a d -> p (a d)")
                        ins = dve.scalar_tensor_tensor(out=row, in0=o_ps[:, t, :], scalar=oscale[:, t:t + 1], in1=row,
                                                       op0=ALU.mult, op1=ALU.add)
                    ins.then_inc(s_x2, 1)
                    wait_alone(dve, s_x2, m + 1)
                    for t in range(KT):
                        row = xa[:, bass.ds(at + t, 1), :].rearrange("p a d -> p (a d)")
                        ins = dve.bn_stats(stats[:, k, t, :], row)
                    ins.then_inc(s_st2, 1)
                    wait_alone(dve, s_st2, m + 1)
                    for t in range(KT):
                        ins = dve.bn_aggr(mv[:, k, t, :], stats[:, k, t, :])
                    ins.then_inc(s_mv, 1)
                if on(n - 2):
                    m = n - 2
                    dve.wait_ge(s_rank, m + 1)
                    dve.tensor_tensor(place[:], rank_ps.rearrange("p (t e) -> p t e", t=KT),
                                      region_of[:].unsqueeze(1).to_broadcast([P, KT, E]), ALU.add).then_inc(s_place, 1)
                    dve.wait_ge(s_place, m + 1)
                    for c in range(TOP_K):
                        ins = dve.tensor_tensor(placed[:, :, c, :], hot[:, :, c, :], place[:], ALU.mult)
                    ins.then_inc(s_placed, 1)
                    dve.wait_ge(s_placed, m + 1)
                    with nc.allow_low_precision(reason="whole numbers below 2 ** 24"):
                        dve.tensor_reduce(slot_i[:, k, :], placed[:].rearrange("p t c e -> p (t c) e"), AX_X,
                                          ALU.add).then_inc(s_slot, 1)
                if on(n - 1) or on(n + 2):
                    dve.wait_ge(s_rstd, n + 3)
                if on(n - 1):
                    m = n - 1
                    if not (isinstance(m, int) and m < 2):
                        dve.wait_ge(s_scat[1 - k], 16 * KT * TOP_K * (i - 1 + k))
                    at_least(dve, s_xn2, m)
                    for t in range(KT):
                        row = xa[:, bass.ds(at + t, 1), :].rearrange("p a d -> p (a d)")
                        for dst in (xn2f[:, t, :], xn2r[:, 1 - k, t, 0:D // 2].bitcast(F16)):
                            ins = dve.tensor_scalar(dst, row, mv[:, k, t, 0:1], rstd[:, k, t:t + 1], ALU.subtract, ALU.mult)
                    ins.then_inc(s_xf, 1)
                if on(n + 2):
                    m = n + 2
                    at = x_at(i + 1, k)
                    at_least(dve, s_t1, m - 1)
                    for t in range(KT):
                        row = xa[:, bass.ds(at + t, 1), :].rearrange("p a d -> p (a d)")
                        ins = dve.tensor_scalar(xn1[:, k, t, :], row, mv[:, k, 2 + t, 0:1], rstd[:, k, 2 + t:3 + t],
                                                ALU.subtract, ALU.mult)
                    ins.then_inc(s_xn1, 1)
                if on(n):
                    dve.wait_ge(s_hi12, n + 1)
                    w = (w1, w2)[k]
                    dve.scalar_tensor_tensor(out=w[1][:, :, bass.ds(i * H, H)], in0=w12_in[:, k], scalar=w_scale[:, 0:1].bitcast(F32),
                                             in1=w[0][:, :, bass.ds(i * H, H)], op0=ALU.mult, op1=ALU.subtract).then_inc(s_lo12, 1)
                    if k == 1:
                        dve.wait_ge(s_hi3, i + 1)
                        dve.scalar_tensor_tensor(out=w3[1][:, :, bass.ds(i * D, D)], in0=w3_in[:], scalar=w_scale[:, 1:2].bitcast(F32),
                                                 in1=w3[0][:, :, bass.ds(i * D, D)], op0=ALU.mult, op1=ALU.subtract).then_inc(s_lo3, 1)
            over_batches(dve, step)

            plan = [0]

            def link(ins):
                plan[0] += 1
                ins.then_inc(s_plan, 1)
                dve.wait_ge(s_plan, plan[0])
            dve.wait_ge(s_cnt, 1)
            link(dve.tensor_copy(cnt[:], cnt_ps))
            link(dve.tensor_tensor(pad_f[:], cnt[0:1, :], region_of[0:1, :], ALU.add))
            dve.tensor_copy(pad_i[:], pad_f[:]).then_inc(s_pad_at, 1)
            link(dve.tensor_scalar(cnt_i[:], cnt[:], float(P - 1), None, ALU.add))
            link(dve.tensor_scalar(full_i[:], cnt_i[:], P.bit_length() - 1, None, ALU.logical_shift_right))
            link(dve.tensor_copy(ntile[:], full_i[:]))
            link(dve.tensor_tensor(ntile_upto[:], upto[:], ntile[:].unsqueeze(1).to_broadcast([P, E, E]), ALU.mult))
            link(dve.tensor_reduce(tile_end[:], ntile_upto[:], AX_X, ALU.add))
            link(dve.tensor_tensor(is_past, tile_end[:].unsqueeze(1).to_broadcast([P, MOE_TILES, E]),
                                   iota_i[:].unsqueeze(2).to_broadcast([P, MOE_TILES, E]), ALU.is_le))
            link(dve.tensor_reduce(tile_e, is_past, AX_X, ALU.add))
            link(dve.tensor_scalar(tile_e, tile_e, float(E - 1), None, ALU.min))
            link(dve.tensor_tensor(past_n, is_past, ntile[:].unsqueeze(1).to_broadcast([P, MOE_TILES, E]), ALU.mult))
            link(dve.tensor_reduce(tile_b, past_n, AX_X, ALU.add))
            link(dve.tensor_tensor(tile_off, iota_i[:], tile_b, ALU.subtract))
            link(dve.tensor_scalar(tile_row, tile_e, float(REGION // P), None, ALU.mult))
            link(dve.tensor_tensor(tile_row, tile_row, tile_off, ALU.add))
            link(dve.tensor_scalar(is_over, iota_i[:], tile_end[:, E - 1:E], None, ALU.is_ge))
            link(dve.tensor_scalar(tile_off[0:1], tile_row[0:1], -float(P), pad_f[0:1, E - 1:E], ALU.mult, ALU.add))
            link(dve.tensor_tensor(tile_off[0:1], tile_off[0:1], is_over[0:1], ALU.mult))
            link(dve.tensor_copy(e_i[:], tile_e[0:1]))
            dve.scalar_tensor_tensor(out=row_i[:], in0=tile_row[0:1], scalar=float(P), in1=tile_off[0:1],
                                     op0=ALU.mult, op1=ALU.add).then_inc(s_map, 1)
            link(dve.tensor_tensor(unscale_y[:], w_unscale[:, 1, :].bitcast(F32), w_unscale[:, 2, :].bitcast(F32), ALU.mult))
            link(dve.tensor_scalar(unscale_y[:], unscale_y[:], tanh_g[:, 1:2], None, ALU.mult))
            link(dve.tensor_tensor(is_past, tile_e.unsqueeze(2).to_broadcast([P, MOE_TILES, E]),
                                   iota_e[:].unsqueeze(1).to_broadcast([P, MOE_TILES, E]), ALU.is_equal))
            link(dve.tensor_tensor(past_n, is_past, w_unscale[:, 0, :].bitcast(F32).unsqueeze(1).to_broadcast([P, MOE_TILES, E]), ALU.mult))
            dve.tensor_reduce(g_unscale[:], past_n, AX_X, ALU.add).then_inc(s_map, 1)
            link(dve.tensor_tensor(y_unscale[:], is_past, unscale_y[:].unsqueeze(1).to_broadcast([P, MOE_TILES, E]), ALU.mult))

            def take_rows(i, k):
                dve.wait_ge(s_xgt, i + 1)
                dve.tensor_copy(xg_t[:, k], xgt_ps).then_inc(s_xgt_copied, 1)
                dve.tensor_tensor(wsel[:, k], xg[:, k, W_AT:W_AT + E],
                                  y_unscale[:, bass.ds(i, 1), :].rearrange("p a e -> p (a e)"), ALU.mult).then_inc(s_wsel, 1)
                dve.wait_ge(s_wsel, i + 1)
                dve.tensor_reduce(wsum[:, k:k + 1], wsel[:, k], AX_X, ALU.add)

            def moe_step(i, j, k, on):
                if on(i - 1):
                    for h in range(2):
                        dve.wait_ge(s_ht_a, 2 * i - 1 + h)
                        rows, cols = (P, slice(0, KF)) if h == 0 else (HL, slice(KF, KH))
                        dve.tensor_tensor(hid_t[1][0:rows, cols, :], ht_ps[h], hid_t[0][0:rows, cols, :], ALU.subtract).then_inc(s_ht_b, 1)
                if on(i + 1):
                    take_rows(i + 1, 1 - k)
                if on(i):
                    dve.wait_ge(s_silu, i + 1)
                    dve.wait_ge(s_u, i + 1)
                    at_least(dve, s_ht, i)
                    dve.tensor_tensor(hid, u_ps, act_g, ALU.mult).then_inc(s_hmul, 1)
                    dve.wait_ge(s_hmul, i + 1)
                    dve.tensor_reduce(h_max[:], hid.rearrange("p b h -> p (b h)"), AX_X, ALU.max,
                                      apply_absolute_value=True).then_inc(s_hmax, 1)
                    dve.wait_ge(s_hmax, i + 1)
                    dve.tensor_scalar(h_cap[:], h_max[:], 2.0 ** -100, None, ALU.max).then_inc(s_hcap, 1)
                    dve.wait_ge(s_hcap, i + 1)
                    dve.tensor_scalar(h_exp[:], h_cap[:].bitcast(I32), 255 * ONE, None, ALU.bitwise_and).then_inc(s_hexp, 1)
                    dve.wait_ge(s_hexp, i + 1)
                    dve.tensor_scalar(h_scale[:], h_exp[:], -1.0, 268.0 * ONE, ALU.mult, ALU.add)
                    dve.tensor_scalar(h_unscale[:], h_exp[:], -14.0 * ONE, None, ALU.add).then_inc(s_hscale, 1)
                    dve.wait_ge(s_hscale, i + 1)
                    dve.tensor_scalar(hid, hid, h_scale[:].bitcast(F32), None, ALU.mult).then_inc(s_h, 1)
                    at_least(dve, s_y_copied, i - 1)
                    dve.tensor_scalar(y_scale[:, k:k + 1], wsum[:, k:k + 1], h_unscale[:].bitcast(F32), None, ALU.mult).then_inc(s_yscale, 1)
                if on(i + 1):
                    if not (isinstance(i, int) and i < 1):
                        dve.wait_ge(s_add[1 - k], 16 * (j + k))
                    dve.tensor_copy(id_s[:, 1 - k:2 - k], xg[:, 1 - k, ID_AT:ID_AT + 1].bitcast(I32)).then_inc(s_meta, 1)
            over_moe_tiles(dve, moe_step)


def kernel(x, ctx_1024, g_xattn, g_ffn, L0_xattn_wq, L0_xattn_wk, L0_xattn_wv, L0_ffn_Wg, L0_ffn_W1, L0_ffn_W2, L0_ffn_W3):
    import concourse.bacc as bacc
    from concourse.bass_utils import run_bass_kernel_spmd

    e, h, d = L0_ffn_W1.shape
    laid = {
        "x": x,
        "ctxT": np.transpose(ctx_1024, (0, 2, 1)),
        "g_xattn": g_xattn,
        "g_ffn": g_ffn,
        "wqT": np.transpose(L0_xattn_wq),
        "wkT": np.transpose(L0_xattn_wk),
        "wv": L0_xattn_wv,
        "WgT": np.transpose(L0_ffn_Wg),
        "W1T": np.transpose(L0_ffn_W1, (2, 0, 1)).reshape(d, e * h),
        "W2T": np.transpose(L0_ffn_W2, (2, 0, 1)).reshape(d, e * h),
        "W3T": np.transpose(L0_ffn_W3, (2, 0, 1)),
    }
    nc = bacc.Bacc("TRN2", target_bir_lowering=False, num_devices=1, dynamic_dma_scratch_size=8192)
    arrays, args = {}, []
    for name, a in laid.items():
        a = np.ascontiguousarray(a)
        arrays[f"in_{name}"] = a
        args.append(nc.dram_tensor(f"in_{name}", a.shape, mybir.dt.from_np(a.dtype), kind="ExternalInput").ap())
    args.append(nc.dram_tensor("out_0", (x.shape[0] * x.shape[1] + P, x.shape[2]), F32, kind="ExternalOutput").ap())
    gated_cross_attention_and_experts(nc, *args)
    r = run_bass_kernel_spmd(nc, [arrays], core_ids=[0])
    return r.results[0]["out_0"][:x.shape[0] * x.shape[1]].reshape(x.shape)
```

```python
from contextlib import ExitStack

import numpy as np

import concourse.bass as bass
from concourse import mybir

ALU = mybir.AluOpType
ACT = mybir.ActivationFunctionType
F32 = mybir.dt.float32
BF16 = mybir.dt.bfloat16
F16 = mybir.dt.float16
I32 = mybir.dt.int32
U32 = mybir.dt.uint32
AX_X = mybir.AxisListType.X

P = 128
EPS = 1e-5
TOP_K = 2
ONE = 1 << 23
XN_EXP = 11


def gated_cross_attention_and_experts(nc, x, ctxT, g_xattn, g_ffn, wqT, wkT, wv, WgT, W1T, W2T, W3T, out):
    B, S, D = x.shape
    E = WgT.shape[1]
    H = W3T.shape[0]
    T = B * S
    KD = D // P
    KT = S // P
    NT = T // P
    KH, KF = 6, 4
    HL = (H - KF * P) // (KH - KF)
    HC = [P] * KF + [HL] * (KH - KF)
    HB = H // 2
    ROW = D + 16
    W_AT, ID_AT = D, D + E
    RING = 8
    REGION = T + P
    MOE_TILES = (TOP_K * T + E * (P - 1)) // P
    BANK = 512
    ARENA = 6656
    PLAN = 5120
    assert S == KT * P and D == KD * P and KT == 2 and KD == 2 and E == 8 and HB <= BANK and B % 2 == 0
    assert sum(HC) == H and KF * P <= BANK and RING % 2 == 0
    assert E * 2 == B

    PARTS = [(0, 0), (1, 0), (0, 1)]
    CONSTS = 2
    UNROLL = 8
    ch = [sum(HC[:c]) for c in range(KH)]
    x_v = x.rearrange("b (t p) d -> b p t d", p=P)
    ctx_v = ctxT.rearrange("b (c p) s -> b p c s", p=P)
    out_v = out[0:T].rearrange("(b t p) d -> b p t d", p=P, t=KT)
    W1_v = W1T.rearrange("(c p) (e h) -> p c e h", p=P, e=E)
    W2_v = W2T.rearrange("(c p) (e h) -> p c e h", p=P, e=E)
    W3_v = W3T[0:KF * P].rearrange("(k p) e d -> p k e d", p=P)
    W3_w = W3T[KF * P:H].rearrange("(k p) e d -> p k e d", p=HL)

    xs = nc.dram_tensor("rows_by_expert", (E * REGION, ROW), F32, kind="Internal").ap()

    with ExitStack() as ctx:
        def sb(name, shape, dt=F32):
            return ctx.enter_context(nc.sbuf_tensor(name, shape, dt))

        def sem(name):
            return ctx.enter_context(nc.semaphore(name))

        psum = ctx.enter_context(nc.psum_tensor("psum", [P, 8, BANK], F32))
        bank = [psum[:, i, :] for i in range(8)]

        arena = ctx.enter_context(nc.sbuf_tensor("arena", [P, ARENA], F32))

        def carve(at, shape, rows=P):
            n = int(np.prod(shape))
            assert at + n <= ARENA
            names = " ".join("abcd"[:len(shape)])
            flat = arena[0:rows, at:at + n]
            if len(shape) == 1:
                return flat
            return flat.rearrange(f"p ({names}) -> p {names}", **dict(zip("abcd", shape)))

        w1 = [sb(f"w1_{n}", [P, KD, E * H], F16) for n in ("hi", "lo")]
        w2 = [sb(f"w2_{n}", [P, KD, E * H], F16) for n in ("hi", "lo")]
        w3 = [sb(f"w3_{n}", [P, KH, E * D], F16) for n in ("hi", "lo")]
        wg = [sb(f"wg_{n}", [P, KD, E], F16) for n in ("hi", "lo")]
        w12_in = sb("w12_in", [P, 2, KD, H])
        w3_in = sb("w3_in", [P, KH, D])
        ssq = sb("ssq", [P, 2])
        rt_unscale = sb("rt_unscale", [P, 1], I32)
        rt_half = sb("rt_half", [P, 1], I32)
        halves = sb("halves", [P, 3, E], I32)
        w_scale = sb("w_scale", [P, 2], I32)
        w_unscale = sb("w_unscale", [P, 3, E], I32)
        wq_t = carve(5120, [KD, D])
        wk_t = carve(5632, [KD, D])
        wv_s = sb("wv_s", [P, KD, D])
        wg_s = sb("wg_s", [P, KD, E])
        qk = sb("qk", [P, KD, D])
        ident = sb("ident", [P, P])
        ident16 = sb("ident16", [P, P], F16)
        ones_f = sb("ones_f", [P, P])
        before = sb("before", [P, P], BF16)
        ones = sb("ones", [P, P], BF16)
        neg_half = sb("neg_half", [P, 4])
        iota_e = sb("iota_e", [P, E])
        region_of = sb("region_of", [P, E])
        token = sb("token", [P, NT], I32)
        iota_i = sb("iota_i", [P, MOE_TILES])
        upto = sb("upto", [P, E, E])
        zrow = sb("zrow", [P, ROW])
        gates = sb("gates", [P, 2])
        tanh_g = sb("tanh_g", [P, 2])
        silu_first = sb("silu_first", [P, 2])
        xa = sb("xa", [P, RING * KT, D])
        xn2r = sb("xn2r", [P, 2, KT, ROW])
        xn2f = carve(0, [KT, D])
        ctx_s = carve(1024, [2, KD, S])
        stats = sb("stats", [P, 2, 4, 6])
        mv = sb("mv", [P, 2, 4, 2])
        var_eps = sb("var_eps", [P, 2, 4])
        rstd = sb("rstd", [P, 2, 4])
        neg_mean = sb("neg_mean", [P, 2, 4])
        shift = sb("shift", [P, 2, 4])
        xn1 = carve(2048, [2, KT, D])
        xn1_t = carve(3072, [KD, S])
        z_s = carve(3584, [KD, S])
        v_s = carve(4096, [2, KT, D])
        nmax = sb("nmax", [P, 2, KT])
        probs = carve(5120, [KT, S])
        sums = sb("sums", [P, 2, KT])
        rsum = sb("rsum", [P, KT])
        probs_t = carve(5632, [KT, S])
        xn2_t = carve(6144, [512]).bitcast(F16).rearrange("p (h c s) -> p h c s", h=2, c=KD)
        top8 = sb("top8", [P, KT, 8])
        idx8 = sb("idx8", [P, KT, 8], U32)
        hot = sb("hot", [P, KT, TOP_K, E])
        mask = sb("mask", [P, KT, E], BF16)
        seen = sb("seen", [P, 2, 2, E], BF16)
        place = sb("place", [P, KT, E])
        placed = sb("placed", [P, KT, TOP_K, E])
        slot_i = sb("slot_i", [P, 2, KT * TOP_K], I32)
        cnt = sb("cnt", [P, E])
        cnt_i = sb("cnt_i", [P, E], I32)
        ntile = sb("ntile", [P, E], I32)
        spare = sb("spare", [P, E])
        ntile_upto = sb("ntile_upto", [P, E, E])
        tile_end = sb("tile_end", [P, E])
        pad_f = sb("pad_f", [1, E])
        pad_i = sb("pad_i", [1, E], I32)
        e_i = sb("e_i", [1, MOE_TILES], I32)
        row_i = sb("row_i", [1, MOE_TILES], I32)
        unscale_y = sb("unscale_y", [P, E])
        g_unscale = sb("g_unscale", [P, MOE_TILES])
        y_unscale = sb("y_unscale", [P, MOE_TILES, E])
        is_past = carve(PLAN, [MOE_TILES, E])
        past_n = carve(PLAN + MOE_TILES * E, [MOE_TILES, E])
        tile_e = carve(PLAN + 2 * MOE_TILES * E, [MOE_TILES])
        tile_row = carve(PLAN + (2 * E + 1) * MOE_TILES, [MOE_TILES])
        xg = carve(0, [2, ROW])
        y_s = carve(2 * ROW, [2, D])
        at = 2 * ROW + 2 * D
        xg_t = carve(at, [2, 2 * KD * P // 2]).bitcast(F16).rearrange("p b (h c s) -> p b h c s", h=2, c=KD)
        act_g = carve(at + 2 * KD * P, [2, HB])
        hid = carve(at + 2 * KD * P + H, [2, HB])
        hid_t = [carve(at + 2 * KD * P + 2 * H + h * KH * P // 2, [KH * P // 2]).bitcast(F16).rearrange("p (c s) -> p c s", c=KH)
                 for h in range(2)]
        wsel = sb("wsel", [P, 2, E])
        wsum = sb("wsum", [P, 2])
        h_max = sb("h_max", [P, 1])
        h_cap = sb("h_cap", [P, 1])
        h_exp = sb("h_exp", [P, 1], I32)
        h_scale = sb("h_scale", [P, 1], I32)
        h_unscale = sb("h_unscale", [P, 1], I32)
        y_scale = sb("y_scale", [P, 2])
        id_s = sb("id_s", [P, 2], I32)

        s_const = sem("s_const")
        s_wqk = sem("s_wqk")
        s_w = sem("s_w")
        s_gate = sem("s_gate")
        s_tanh = sem("s_tanh")
        s_qk = sem("s_qk")
        s_qk_copied = sem("s_qk_copied")
        s_w12 = [sem(f"s_w12_{k}") for k in range(2)]
        s_w3 = sem("s_w3")
        s_sq = sem("s_sq")
        s_ssq = sem("s_ssq")
        s_half = sem("s_half")
        s_scale = sem("s_scale")
        s_hi12 = sem("s_hi12")
        s_hi3 = sem("s_hi3")
        s_lo12 = sem("s_lo12")
        s_lo3 = sem("s_lo3")
        s_wg = sem("s_wg")
        s_pool = sem("s_pool")
        s_x2st = [sem(f"s_x2st{k}") for k in range(2)]
        s_xf = sem("s_xf")
        s_xh = sem("s_xh")
        s_pow = sem("s_pow")
        s_dummy = sem("s_dummy")
        s_x = [sem(f"s_x{k}") for k in range(2)]
        s_ctx = [sem(f"s_ctx{k}") for k in range(2)]
        s_st1 = sem("s_st1")
        s_st2 = sem("s_st2")
        s_mv = sem("s_mv")
        s_ve = sem("s_ve")
        s_rstd = sem("s_rstd")
        s_xn1 = sem("s_xn1")
        s_xn2 = sem("s_xn2")
        s_t1 = sem("s_t1")
        s_t1_copied = sem("s_t1_copied")
        s_z = sem("s_z")
        s_z_copied = sem("s_z_copied")
        s_v = sem("s_v")
        s_v_copied = sem("s_v_copied")
        s_sc = sem("s_sc")
        s_max = sem("s_max")
        s_exp = sem("s_exp")
        s_pt = sem("s_pt")
        s_pt_copied = sem("s_pt_copied")
        s_rsum = sem("s_rsum")
        s_pv = sem("s_pv")
        s_x2 = sem("s_x2")
        s_t2 = sem("s_t2")
        s_t2_copied = sem("s_t2_copied")
        s_rt = sem("s_rt")
        s_rcopy = sem("s_rcopy")
        s_top = sem("s_top")
        s_idx = sem("s_idx")
        s_hot = sem("s_hot")
        s_mask = sem("s_mask")
        s_seen1 = sem("s_seen1")
        s_seen = sem("s_seen")
        s_rank = sem("s_rank")
        s_place = sem("s_place")
        s_placed = sem("s_placed")
        s_slot = sem("s_slot")
        s_scat = [sem(f"s_scat{k}") for k in range(2)]
        s_cnt = sem("s_cnt")
        s_plan = sem("s_plan")
        s_pad_at = sem("s_pad_at")
        s_map = sem("s_map")
        s_pad = sem("s_pad")
        s_xg = [sem(f"s_xg{k}") for k in range(2)]
        s_xgt = sem("s_xgt")
        s_xgt_copied = sem("s_xgt_copied")
        s_g = sem("s_g")
        s_u = sem("s_u")
        s_silu = sem("s_silu")
        s_h = sem("s_h")
        s_ht = sem("s_ht")
        s_ht_a = sem("s_ht_a")
        s_ht_b = sem("s_ht_b")
        s_y = sem("s_y")
        s_y_copied = sem("s_y_copied")
        s_meta = sem("s_meta")
        s_wsel = sem("s_wsel")
        s_hmul = sem("s_hmul")
        s_hmax = sem("s_hmax")
        s_hcap = sem("s_hcap")
        s_hexp = sem("s_hexp")
        s_hscale = sem("s_hscale")
        s_yscale = sem("s_yscale")
        s_add = [sem(f"s_add{k}") for k in range(2)]

        t1_ps = bank[0].rearrange("p (c s) -> p c s", c=KD)
        z_ps = bank[1].rearrange("p (c s) -> p c s", c=KD)
        v_ps = bank[2].rearrange("p (t d) -> p t d", t=KT)
        sc_ps = bank[3].rearrange("p (t s) -> p t s", t=KT)
        pt_ps = bank[4].rearrange("p (t s) -> p t s", t=KT)
        o_ps = bank[5].rearrange("p (t d) -> p t d", t=KT)
        t2_ps = bank[6].bitcast(F16).rearrange("p (h c s) -> p h c s", h=2, c=KD)
        rt_ps = bank[7][:, 0:KT * E]
        rank_ps = bank[7][:, 64:64 + KT * E]
        cnt_ps = bank[7][:, 128:128 + E]
        ssq_ps = bank[7][:, 192:194]
        g_ps = psum[:, 0:2, 0:HB]
        u_ps = psum[:, 2:4, 0:HB]
        ht_ps = [bank[4].rearrange("p (c s) -> p c s", c=KF), bank[5][0:HL, 0:2 * P].rearrange("p (c s) -> p c s", c=2)]
        xgt_ps = bank[6][:, 0:KD * P].bitcast(F16).rearrange("p (h c s) -> p h c s", h=2, c=KD)
        y_ps = bank[7][:, 0:D]

        def at_least(eng, s, v):
            if not (isinstance(v, int) and v <= 0):
                eng.wait_ge(s, v)

        def wait_alone(eng, s, v):
            if not (isinstance(v, int) and v <= 0):
                if not isinstance(v, int):
                    v = eng.to_reg(v)
                eng.wait_ge(s_const, CONSTS)
                eng.wait_ge(s, v)

        def x_at(i, k):
            return KT * (2 * (i % (RING // 2)) + k)

        def over_batches(eng, step):
            def peeled(n):
                step(n, n // 2, n % 2, lambda m: 0 <= m < B)
            for n in range(-2, 4):
                peeled(n)
            with eng.Fori(2, B // 2 - 1) as i:
                for k in range(2):
                    step(2 * i + k, i, k, lambda m: True)
            for n in range(B - 2, B + 3):
                peeled(n)

        def over_moe_tiles(eng, step, before=lambda i, n: None):
            def peeled(i):
                before(i, 1)
                step(i, i // 2, i % 2, lambda m: 0 <= m < MOE_TILES)
            first = 4
            turns = (MOE_TILES - 1 - first) // UNROLL
            last = first + turns * UNROLL
            for i in range(-1, first):
                peeled(i)
            with eng.Fori(0, turns) as r:
                before(UNROLL * r + first, UNROLL)
                for u in range(first, first + UNROLL):
                    step(UNROLL * r + u, UNROLL // 2 * r + u // 2, u % 2, lambda m: True)
            for i in range(last, MOE_TILES + 1):
                peeled(i)

        block = ctx.enter_context(nc.Block())

        @block.sync
        def _(sp):
            def load_x(m, i, k):
                at_least(sp, s_st1, m - 1)
                at_least(sp, s_x2st[k], 16 * (i - RING // 2 + 1))
                row = x_v[bass.ds(m, 1)].rearrange("a p t d -> (a p) t d")
                sp.dma_start(xa[:, bass.ds(x_at(i, k), KT), :], row).then_inc(s_x[k], 16)

            def load_ctx(m, k):
                at_least(sp, s_v, m - 1)
                row = ctx_v[bass.ds(m, 1)].rearrange("a p c s -> (a p) c s")
                sp.dma_start(ctx_s[:, k], row).then_inc(s_ctx[k], 16)

            def load_w12(m, e, k):
                at_least(sp, s_lo12, m - 1)
                src = (W1_v, W2_v)[k][:, :, bass.ds(e, 1), :].rearrange("p c e h -> p c (e h)")
                sp.dma_start(w12_in[:, k], src).then_inc(s_w12[k], 16)

            def load_w3(e):
                at_least(sp, s_lo3, e)
                sp.dma_start(w3_in[:, 0:KF, :], W3_v[:, :, bass.ds(e, 1), :].rearrange("p k e d -> p k (e d)")).then_inc(s_w3, 16)
                sp.dma_start(w3_in[0:HL, KF:KH, :], W3_w[:, :, bass.ds(e, 1), :].rearrange("p k e d -> p k (e d)")).then_inc(s_w3, 16)

            load_x(0, 0, 0)
            sp.dma_start(wq_t, wqT.rearrange("(c p) d -> p c d", p=P)).then_inc(s_wqk, 16)
            sp.dma_start(wk_t, wkT.rearrange("(c p) d -> p c d", p=P)).then_inc(s_wqk, 16)
            load_ctx(0, 0)
            sp.dma_start(wv_s[:], wv.rearrange("(c p) d -> p c d", p=P)).then_inc(s_w, 16)
            load_x(1, 0, 1)
            sp.dma_start(wg_s[:], WgT.rearrange("(c p) e -> p c e", p=P)).then_inc(s_w, 16)
            with nc.allow_non_contiguous_dma(reason="one gate to every partition"):
                sp.dma_start(gates[:, 0:1], g_xattn.rearrange("(a n) -> a n", a=1).to_broadcast([P, 1])).then_inc(s_gate, 16)
                sp.dma_start(gates[:, 1:2], g_ffn.rearrange("(a n) -> a n", a=1).to_broadcast([P, 1])).then_inc(s_gate, 16)
            load_w12(0, 0, 0)
            sp.wait_ge(s_const, CONSTS)
            sp.dma_start(out[T:T + P, :], zrow[:, 0:D]).then_inc(s_dummy, 16)

            load_x(2, 1, 0)
            load_x(3, 1, 1)
            load_ctx(1, 1)

            def step(m, i, k, on):
                if on(m + 4):
                    load_x(m + 4, i + 2, k)
                if on(m + 2):
                    load_ctx(m + 2, k)
                if on(m + 1):
                    load_w12(m + 1, i + k, 1 - k)
                if k == 0:
                    load_w3(i)
            for m in range(6):
                step(m, m // 2, m % 2, lambda m: True)
            with sp.Fori(3, B // 2 - 2) as i:
                for k in range(2):
                    step(2 * i + k, i, k, lambda m: True)
            for m in range(B - 4, B):
                step(m, m // 2, m % 2, lambda m: m < B)

            sp.wait_ge(s_pad_at, 1)
            pad_at = [sp.alloc_register(f"pad_at_{e}") for e in range(E)]
            sp.load(pad_at, pad_i[0:1, :])
            for e in range(E):
                at = sp.snap(pad_at[e], min_val=e * REGION, max_val=e * REGION + T)
                sp.dma_start(xs[bass.ds(at, P), :], zrow[:]).then_inc(s_pad, 16)
            for k in range(2):
                sp.wait_ge(s_scat[k], 16 * KT * TOP_K * (B // 2))
            sp.wait_ge(s_pad, 16 * E)
            sp.wait_ge(s_map, 1)

            def load_rows(i, k):
                at_least(sp, s_xgt, i - 1)
                at_least(sp, s_meta, i - 1)
                at = sp.value_load(row_i[0:1, bass.ds(i, 1)], min_val=0, max_val=E * REGION - P)
                sp.dma_start(xg[:, k, :], xs[bass.ds(at, P), :]).then_inc(s_xg[k], 16)

            load_rows(0, 0)
            load_rows(1, 1)
            load_rows(2, 0)
            load_rows(3, 1)
            with sp.Fori(2, MOE_TILES // 2) as j:
                for k in range(2):
                    load_rows(2 * j + k, k)
            for i in range(MOE_TILES - MOE_TILES % 2, MOE_TILES):
                load_rows(i, i % 2)
            for k in range(2):
                sp.wait_ge(s_add[k], 16 * ((MOE_TILES + 1 - k) // 2))

        @block.gpsimd
        def _(pool):
            pool.memset(ident[:], 0.0).then_inc(s_pool, 1)
            pool.memset(ones[:], 1.0).then_inc(s_pool, 1)
            pool.memset(zrow[:], 0.0).then_inc(s_pool, 1)
            pool.memset(upto[:], 1.0).then_inc(s_pool, 1)
            pool.wait_ge(s_pool, 4)
            pool.affine_select(out=ident[:], in_=ident[:], compare_op=ALU.not_equal, fill=1.0, base=0,
                               pattern=[[-1, P]], channel_multiplier=1).then_inc(s_pool, 1)
            pool.affine_select(out=before[:], in_=ones[:], compare_op=ALU.is_gt, fill=0.0, base=0,
                               pattern=[[1, P]], channel_multiplier=-1)
            pool.affine_select(out=upto[:], in_=upto[:], compare_op=ALU.is_ge, fill=0.0, base=0,
                               pattern=[[1, E], [-1, E]], channel_multiplier=0)
            pool.iota(zrow[:, ID_AT:ID_AT + 1].bitcast(I32), [[0, 1]], base=T, channel_multiplier=1)
            pool.memset(neg_half[:], -0.5)
            pool.memset(ones_f[:], 1.0)
            pool.memset(seen[:], 0.0)
            pool.memset(xn2r[:], 0.0)
            pool.memset(w3_in[:], 0.0)
            pool.wait_ge(s_pool, 5)
            pool.tensor_copy(ident16[:], ident[:])
            pool.iota(token[:], [[P, NT]], base=0, channel_multiplier=1)
            pool.iota(iota_e[:], [[1, E]], base=0, channel_multiplier=0, allow_small_or_imprecise_dtypes=True)
            pool.iota(region_of[:], [[REGION, E]], base=0, channel_multiplier=0, allow_small_or_imprecise_dtypes=True)
            pool.iota(iota_i[:], [[1, MOE_TILES]], base=0, channel_multiplier=0,
                      allow_small_or_imprecise_dtypes=True).then_inc(s_const, CONSTS)

            def step(n, i, k, on):
                if on(n - 2):
                    pool.wait_ge(s_xh, n - 1)
                    pool.wait_ge(s_xf, n - 1)
                    pool.tensor_tensor(xn2r[:, k, :, D // 2:D].bitcast(F16), xn2f,
                                       xn2r[:, k, :, 0:D // 2].bitcast(F16), ALU.subtract).then_inc(s_xn2, 1)
                if on(n - 3):
                    wait_alone(pool, s_slot, n - 2)
                    for t in range(KT):
                        for c in range(TOP_K):
                            col = t * TOP_K + c
                            pool.indirect_dma_start(
                                out=xs[:, :], out_offset=bass.IndirectOffsetOnAxis(ap=slot_i[:, 1 - k, col:col + 1], axis=0),
                                in_=xn2r[:, 1 - k, t, :], in_offset=None).then_inc(s_scat[1 - k], 16)
                a, b = (0 if on(n - 1) else 2), (4 if on(n + 2) else 2)
                if a < b:
                    if on(n):
                        pool.wait_ge(s_xn1, n + 1)
                    wait_alone(pool, s_mv, n + 3)
                if on(n - 1):
                    pool.tensor_scalar(var_eps[:, k, 0:2], mv[:, k, 0:2, 1], EPS, 2.0 ** (-2 * XN_EXP), ALU.add, ALU.mult)
                if on(n + 2):
                    pool.tensor_scalar(var_eps[:, k, 2:4], mv[:, k, 2:4, 1], EPS, None, ALU.add)
                if a < b:
                    pool.tensor_scalar(neg_mean[:, k, a:b], mv[:, k, a:b, 0], -1.0, None, ALU.mult).then_inc(s_ve, 1)
                    pool.wait_ge(s_ve, n + 3)
                    pool.tensor_tensor(rstd[:, k, a:b], var_eps[:, k, a:b], neg_half[:, a:b], ALU.pow).then_inc(s_pow, 1)
                    pool.wait_ge(s_pow, n + 3)
                    pool.tensor_tensor(shift[:, k, a:b], neg_mean[:, k, a:b], rstd[:, k, a:b], ALU.mult).then_inc(s_rstd, 1)
            over_batches(pool, step)

            for k in range(2):
                pool.wait_ge(s_x2st[k], 16 * (B // 2))
            pool.wait_ge(s_dummy, 16)

            def add_rows(i, j, k):
                if k == 0:
                    if not (isinstance(i, int) and i == 0):
                        pool.wait_ge(s_add[1], 16 * j)
                else:
                    pool.wait_ge(s_add[0], 16 * j + 16)
                wait_alone(pool, s_y_copied, i + 1)
                pool.indirect_dma_start(
                    out=out[:, :], out_offset=bass.IndirectOffsetOnAxis(ap=id_s[:, k:k + 1], axis=0),
                    in_=y_s[:, k, :], in_offset=None, compute_op=ALU.add).then_inc(s_add[k], 16)
            add_rows(0, 0, 0)
            add_rows(1, 0, 1)
            with pool.Fori(1, MOE_TILES // 2) as j:
                for k in range(2):
                    add_rows(2 * j + k, j, k)
            for i in range(MOE_TILES - MOE_TILES % 2, MOE_TILES):
                add_rows(i, i // 2, i % 2)

        @block.scalar
        def _(act):
            act.wait_ge(s_qk, 1)
            act.activation(qk[:], z_ps, ACT.Copy).then_inc(s_qk_copied, 1)

            def norm(dst, at, t, col):
                return act.activation(dst, xa[:, bass.ds(at + t, 1), :].rearrange("p a d -> p (a d)"), ACT.Identity,
                                      scale=rstd[:, col[0], col[1] + t:col[1] + t + 1], bias=shift[:, col[0], col[1] + t:col[1] + t + 1])

            def router_weights(n):
                if isinstance(n, int) and n == 0:
                    act.wait_ge(s_gate, 32)
                    act.activation(tanh_g[:], gates[:], ACT.Tanh).then_inc(s_tanh, 1)
                    act.wait_ge(s_w, 32)
                    act.activation(wg[0][:].bitcast(BF16), wg_s[:], ACT.Square, accum_out=ssq[:, 0:1]).then_inc(s_sq, 1)
                    act.wait_ge(s_tanh, 1)
                if isinstance(n, int) and n == 1:
                    act.wait_ge(s_scale, 1)
                    act.activation(wg[0][:], wg_s[:], ACT.Copy, scale=w_scale[:, 0:1].bitcast(F32)).then_inc(s_wg, 1)

            def step(n, i, k, on):
                router_weights(n)
                if on(n):
                    act.wait_ge(s_z, n + 1)
                    act.activation(z_s, z_ps, ACT.Copy).then_inc(s_z_copied, 1)
                if on(n):
                    act.wait_ge(s_v, n + 1)
                    act.activation(v_s[:, k], v_ps, ACT.Copy, scale=tanh_g[:, 0:1]).then_inc(s_v_copied, 1)
                if on(n - 1):
                    act.wait_ge(s_pt, n)
                    act.activation(probs_t, pt_ps, ACT.Copy).then_inc(s_pt_copied, 1)
                if on(n - 2) or on(n + 1):
                    wait_alone(act, s_rstd, n + 2)
                if on(n - 2):
                    if not (isinstance(n, int) and n < 3):
                        wait_alone(act, s_xn2, n - 2)
                    for t in range(KT):
                        ins = norm(xn2f[:, t, :], x_at(i - 1, k), t, (1 - k, 0))
                    ins.then_inc(s_xf, 1)
                if on(n + 1):
                    if not (isinstance(n, int) and n < 1):
                        wait_alone(act, s_t1, n)
                    for t in range(KT):
                        ins = norm(xn1[:, 1 - k, t, :], x_at(i + k, 1 - k), t, (1 - k, 2))
                    ins.then_inc(s_xn1, 1)
                if on(n - 1):
                    wait_alone(act, s_scale, n + 1)
                    e = i - 1 + k
                    act.activation((w1, w2)[1 - k][0][:, :, bass.ds(e * H, H)], w12_in[:, 1 - k], ACT.Copy,
                                   scale=w_scale[:, 0:1].bitcast(F32)).then_inc(s_hi12, 1)
                if on(n - 2):
                    act.wait_ge(s_t2, n - 1)
                    act.activation(xn2_t, t2_ps, ACT.Copy).then_inc(s_t2_copied, 1)
                    act.wait_ge(s_x2, n - 1)
                    at_least(act, s_x2st[k], 16 * (i - 1))
                    act.dma_start(out_v[bass.ds(n - 2, 1)].rearrange("a p t d -> (a p) t d"),
                                  xa[:, bass.ds(x_at(i - 1, k), KT), :]).then_inc(s_x2st[k], 16)
                if on(n):
                    act.wait_ge(s_max, n + 1)
                    for t in range(KT):
                        ins = act.activation(probs[:, t, :], sc_ps[:, t, :], ACT.Exp, bias=nmax[:, k, t:t + 1],
                                             accum_out=sums[:, k, t:t + 1])
                    ins.then_inc(s_exp, 1)
                if on(n - 1) and k == 0:
                    act.activation(w3[0][:, :, bass.ds(e * D, D)], w3_in[:], ACT.Copy,
                                   scale=w_scale[:, 1:2].bitcast(F32)).then_inc(s_hi3, 1)
                if on(n + 1):
                    act.wait_ge(s_t1, n + 2)
                    act.activation(xn1_t, t1_ps, ACT.Copy).then_inc(s_t1_copied, 1)
                if on(n):
                    act.wait_ge(s_w12[k], 16 * i + 16)
                    wait_alone(act, s_ssq, n + 1)
                    ins = act.activation((w1, w2)[k][0][:, :, bass.ds(i * H, H)].bitcast(BF16), w12_in[:, k], ACT.Square,
                                         accum_out=ssq[:, 0:1])
                    if k == 1:
                        wait_alone(act, s_w3, 32 * i + 32)
                        ins = act.activation(w3[0][:, :, bass.ds(i * D, D)].bitcast(BF16), w3_in[:], ACT.Square,
                                             accum_out=ssq[:, 1:2])
                    ins.then_inc(s_sq, 1)
            over_batches(act, step)

            act.activation(silu_first[:], tanh_g[:], ACT.Silu)
            act.wait_ge(s_map, 2)

            def moe_step(i, j, k, on):
                if on(i):
                    act.wait_ge(s_g, i + 1)
                    at_least(act, s_hmul, i)
                    act.activation(act_g, g_ps, ACT.Silu, scale=g_unscale[:, bass.ds(i, 1)]).then_inc(s_silu, 1)
                if on(i - 1):
                    act.wait_ge(s_ht, i)
                    act.activation(hid_t[0][:, 0:KF, :], ht_ps[0], ACT.Copy).then_inc(s_ht_a, 1)
                    act.activation(hid_t[0][0:HL, KF:KH, :], ht_ps[1], ACT.Copy).then_inc(s_ht_a, 1)
                    act.wait_ge(s_y, i)
                    act.wait_ge(s_yscale, i)
                    if not (isinstance(i, int) and i < 3):
                        act.wait_ge(s_add[1 - k], 16 * (j - 1 + k))
                    act.activation(y_s[:, 1 - k, :], y_ps, ACT.Copy, scale=y_scale[:, 1 - k:2 - k]).then_inc(s_y_copied, 1)
            over_moe_tiles(act, moe_step)

        @block.tensor
        def _(pe):
            pe.wait_ge(s_wqk, 32)
            for i in range(KD):
                for h in range(KD):
                    ins = pe.matmul(z_ps[:, i, :], wk_t[:, h, i * P:(i + 1) * P], wq_t[:, h, :],
                                    start=(h == 0), stop=(h == KD - 1))
            ins.then_inc(s_qk, 1)
            pe.wait_ge(s_const, CONSTS)

            def turn(dst, src, rows, cols, ident=ident):
                for c in range(cols):
                    for t in range(rows):
                        ins = pe.transpose(dst[:, c, t * P:(t + 1) * P], src[:, t, c * P:(c + 1) * P], ident[:])
                return ins

            def product(dst, left, right):
                for t in range(2):
                    for c in range(2):
                        ins = pe.matmul(dst[:, t, :], left[:, c, t * P:(t + 1) * P], right[:, c, :],
                                        start=(c == 0), stop=(c == 1))
                return ins

            def step(n, i, k, on):
                if on(n):
                    if isinstance(n, int) and n == 0:
                        pe.wait_ge(s_qk_copied, 1)
                    pe.wait_ge(s_ctx[k], 16 * i + 16)
                    at_least(pe, s_z_copied, n)
                    product(z_ps, qk, ctx_s[:, k]).then_inc(s_z, 1)
                    at_least(pe, s_v_copied, n)
                    if isinstance(n, int) and n == 0:
                        pe.wait_ge(s_w, 32)
                    product(v_ps, ctx_s[:, k], wv_s).then_inc(s_v, 1)
                if isinstance(n, int) and n == 0:
                    pe.wait_ge(s_sq, 1)
                    pe.matmul(ssq_ps[:, 0:1], ones_f[:], ssq[:, 0:1], start=True, stop=True).then_inc(s_ssq, 1)
                if on(n - 1):
                    pe.wait_ge(s_exp, n)
                    at_least(pe, s_pt_copied, n - 1)
                    turn(pt_ps, probs, KT, KT).then_inc(s_pt, 1)
                if on(n - 3):
                    pe.wait_ge(s_seen1, n - 2)
                    pe.wait_ge(s_rcopy, n - 2)
                    pe.matmul(rank_ps, before[:], mask[:].rearrange("p t e -> p (t e)"), start=True, stop=False)
                    pe.matmul(rank_ps, ones[:], seen[:, 1 - k].rearrange("p t e -> p (t e)"),
                              start=False, stop=True).then_inc(s_rank, 1)
                if on(n - 1):
                    pe.wait_ge(s_sq, n + 1)
                    w = 2 - k
                    pe.matmul(ssq_ps[:, 0:w], ones_f[:], ssq[:, 0:w], start=True, stop=True).then_inc(s_ssq, 1)
                if on(n):
                    pe.wait_ge(s_z_copied, n + 1)
                    pe.wait_ge(s_t1_copied, n + 1)
                    product(sc_ps, xn1_t, z_s).then_inc(s_sc, 1)
                if on(n - 1):
                    pe.wait_ge(s_pt_copied, n)
                    pe.wait_ge(s_v_copied, n)
                    at_least(pe, s_x2, n - 1)
                    product(o_ps, probs_t, v_s[:, 1 - k]).then_inc(s_pv, 1)
                if on(n - 2):
                    pe.wait_ge(s_xn2, n - 1)
                    at_least(pe, s_t2_copied, n - 2)
                    for h in range(2):
                        ins = turn(t2_ps[:, h], xn2r[:, k, :, h * D // 2:(h + 1) * D // 2].bitcast(F16), KT, KD, ident16)
                    ins.then_inc(s_t2, 1)
                if on(n + 1):
                    pe.wait_ge(s_xn1, n + 2)
                    at_least(pe, s_t1_copied, n + 1)
                    turn(t1_ps, xn1[:, 1 - k], KT, KD).then_inc(s_t1, 1)
                if on(n - 2):
                    pe.wait_ge(s_t2_copied, n - 1)
                    at_least(pe, s_place, n - 2)
                    if on(n - 1):
                        pe.wait_ge(s_scale, n + 1)
                    pe.wait_ge(s_wg, 2)
                    for t in range(KT):
                        for q, (a, b) in enumerate(PARTS):
                            for c in range(KD):
                                ins = pe.matmul(rt_ps[:, t * E:(t + 1) * E], xn2_t[:, a, c, t * P:(t + 1) * P], wg[b][:, c, :],
                                                start=(q == 0 and c == 0), stop=(q == 2 and c == KD - 1))
                    ins.then_inc(s_rt, 1)
            over_batches(pe, step)

            pe.wait_ge(s_seen, B)
            pe.wait_ge(s_place, B)
            pe.matmul(cnt_ps, ones[:], seen[:, 0, 0, :], start=True, stop=True).then_inc(s_cnt, 1)

            pe.wait_ge(s_lo12, 2 * E)
            pe.wait_ge(s_lo3, E)
            pe.wait_ge(s_map, 1)

            def turn_rows(i, j, k):
                pe.wait_ge(s_xg[k], 16 * j + 16)
                at_least(pe, s_xgt_copied, i)
                for h in range(2):
                    for c in range(KD):
                        ins = pe.transpose(xgt_ps[:, h, c, :], xg[:, k, h * D // 2 + c * P // 2:h * D // 2 + (c + 1) * P // 2].bitcast(F16),
                                           ident16[:])
                ins.then_inc(s_xgt, 1)

            def to_hidden(ps, w, e, k):
                for b in range(2):
                    for q, (x_part, w_part) in enumerate(PARTS):
                        for c in range(KD):
                            ins = pe.matmul(ps[:, b, :], xg_t[:, k, x_part, c, :], w[w_part][:, c, bass.ds(e * H + b * HB, HB)],
                                            start=(q == 0 and c == 0), stop=(q == 2 and c == KD - 1))
                return ins

            held = [pe.alloc_register(f"expert_{u}") for u in range(UNROLL)]
            last_held = pe.alloc_register("expert_before")
            expert = {}
            pe.reg_mov(held[-1], 0)

            def take_experts(i, n):
                pe.reg_mov(last_held, held[-1])
                if not isinstance(i, int) or 0 <= i < MOE_TILES:
                    pe.load(held[UNROLL - n:], e_i[0:1, bass.ds(i, n)])
                for u in range(-1, n):
                    reg = last_held if u < 0 else held[UNROLL - n + u]
                    expert[u] = pe.snap(reg, min_val=0, max_val=E - 1)
                expert["step"] = 0

            def moe_step(i, j, k, on):
                e, e1 = expert[expert["step"]], expert[expert["step"] - 1]
                expert["step"] += 1
                if on(i):
                    pe.wait_ge(s_xgt_copied, i + 1)
                    at_least(pe, s_silu, i)
                    to_hidden(g_ps, w1, e, k).then_inc(s_g, 1)
                if on(i - 1):
                    pe.wait_ge(s_h, i)
                    at_least(pe, s_ht_b, 2 * i - 2)
                    for c in range(KH):
                        dst = ht_ps[0][:, c, :] if c < KF else ht_ps[1][:, c - KF, :]
                        flat = hid.rearrange("p b h -> p (b h)")
                        ins = pe.transpose(dst, flat[:, ch[c]:ch[c] + HC[c]], ident[:])
                    ins.then_inc(s_ht, 1)
                if on(i + 1):
                    turn_rows(i + 1, j + k, 1 - k)
                if on(i):
                    at_least(pe, s_hmul, i)
                    to_hidden(u_ps, w2, e, k).then_inc(s_u, 1)
                if on(i - 1):
                    pe.wait_ge(s_ht_b, 2 * i)
                    at_least(pe, s_y_copied, i - 1)
                    for q, (h_part, w_part) in enumerate(PARTS):
                        for c in range(KH):
                            ins = pe.matmul(y_ps, hid_t[h_part][0:HC[c], c, :], w3[w_part][0:HC[c], c, bass.ds(e1 * D, D)],
                                            start=(q == 0 and c == 0), stop=(q == 2 and c == KH - 1))
                    ins.then_inc(s_y, 1)
            over_moe_tiles(pe, moe_step, take_experts)

        @block.vector
        def _(dve):
            dve.wait_ge(s_const, CONSTS)

            def scales(half_exp, w, n):
                dve.tensor_scalar(half_exp, ssq_ps[:, 0:w].bitcast(I32), 24, None,
                                  ALU.logical_shift_right).then_inc(s_half, 1)
                dve.wait_ge(s_half, n + 2)
                dve.tensor_scalar(w_scale[:, 0:w], half_exp, -float(ONE), 203.0 * ONE, ALU.mult,
                                  ALU.add).then_inc(s_scale, 1)

            def unscale(dst, half_exp, less):
                return dve.tensor_scalar(dst, half_exp, float(ONE), float((51 - less) * ONE), ALU.mult, ALU.add)

            def router_weights(n):
                if isinstance(n, int) and n == 0:
                    dve.wait_ge(s_ssq, 1)
                    scales(rt_half[:], 1, -1)
                    unscale(rt_unscale[:], rt_half[:], XN_EXP)
                if isinstance(n, int) and n == 1:
                    dve.wait_ge(s_scale, 1)
                    dve.wait_ge(s_wg, 1)
                    dve.scalar_tensor_tensor(out=wg[1][:], in0=wg_s[:], scalar=w_scale[:, 0:1].bitcast(F32), in1=wg[0][:],
                                             op0=ALU.mult, op1=ALU.subtract).then_inc(s_wg, 1)

            def tile(at, t):
                return xa[:, bass.ds(at + t, 1), :].rearrange("p a d -> p (a d)")

            def lo12(k, e, c):
                w = (w1, w2)[1 - k]
                return dve.scalar_tensor_tensor(out=w[1][:, c:c + 1, bass.ds(e * H, H)], in0=w12_in[:, 1 - k, c:c + 1],
                                                scalar=w_scale[:, 0:1].bitcast(F32), in1=w[0][:, c:c + 1, bass.ds(e * H, H)],
                                                op0=ALU.mult, op1=ALU.subtract)

            def lo3(e):
                return dve.scalar_tensor_tensor(out=w3[1][:, :, bass.ds(e * D, D)], in0=w3_in[:], scalar=w_scale[:, 1:2].bitcast(F32),
                                                in1=w3[0][:, :, bass.ds(e * D, D)], op0=ALU.mult, op1=ALU.subtract)

            def step(n, i, k, on):
                router_weights(n)
                if on(n - 2) or on(n + 1):
                    dve.wait_ge(s_rstd, n + 2)
                if on(n - 2):
                    m, at = n - 2, x_at(i - 1, k)
                    at_least(dve, s_scat[k], 16 * KT * TOP_K * (i - 1))
                    for t in range(KT):
                        ins = dve.tensor_scalar(xn2r[:, k, t, 0:D // 2].bitcast(F16), tile(at, t), mv[:, 1 - k, t, 0:1],
                                                rstd[:, 1 - k, t:t + 1], ALU.subtract, ALU.mult)
                    ins.then_inc(s_xh, 1)
                if on(n - 1):
                    dve.wait_ge(s_ssq, n + 1)
                if on(n - 3):
                    m = n - 3
                    dve.wait_ge(s_rank, m + 1)
                    dve.tensor_tensor(place[:], rank_ps.rearrange("p (t e) -> p t e", t=KT),
                                      region_of[:].unsqueeze(1).to_broadcast([P, KT, E]), ALU.add).then_inc(s_place, 1)
                    dve.wait_ge(s_place, m + 1)
                    for c in range(TOP_K):
                        ins = dve.tensor_tensor(placed[:, :, c, :], hot[:, :, c, :], place[:], ALU.mult)
                    ins.then_inc(s_placed, 1)
                    dve.wait_ge(s_placed, m + 1)
                    with nc.allow_low_precision(reason="whole numbers below 2 ** 24"):
                        dve.tensor_reduce(slot_i[:, 1 - k, :], placed[:].rearrange("p t c e -> p (t c) e"), AX_X,
                                          ALU.add).then_inc(s_slot, 1)
                if isinstance(n, int) and n == B + 1:
                    dve.wait_ge(s_hi12, B)
                    lo12(0, E - 1, 0)
                    lo12(0, E - 1, 1).then_inc(s_lo12, 1)
                    dve.wait_ge(s_hi3, E)
                    lo3(E - 1).then_inc(s_lo3, 1)
                if on(n - 1):
                    e = i - 1 + k
                    half_exp = halves[:, 1 - k:3 - 2 * k, bass.ds(e, 1)].rearrange("p m a -> p (m a)")
                    scales(half_exp, 2 - k, n - 1)
                if on(n + 2):
                    m = n + 2
                    at = x_at(i + 1, k)
                    wait_alone(dve, s_x[k], 16 * (i + 1) + 16)
                    for t in range(KT):
                        ins = dve.bn_stats(stats[:, k, 2 + t, :], tile(at, t))
                    ins.then_inc(s_st1, 1)
                    wait_alone(dve, s_st1, m + 1)
                    for t in range(KT):
                        ins = dve.bn_aggr(mv[:, k, 2 + t, :], stats[:, k, 2 + t, :])
                    if not on(n - 1):
                        ins.then_inc(s_mv, 1)
                if on(n - 1):
                    dve.wait_ge(s_exp, n)
                    dve.reciprocal(rsum[:], sums[:, 1 - k, :]).then_inc(s_rsum, 1)
                if on(n):
                    dve.wait_ge(s_sc, n + 1)
                    dve.tensor_reduce(nmax[:, k, :], sc_ps, AX_X, ALU.max, negate=True).then_inc(s_max, 1)
                if on(n - 1):
                    m, at = n - 1, x_at(i - 1 + k, 1 - k)
                    dve.wait_ge(s_rsum, m + 1)
                    dve.wait_ge(s_pv, m + 1)
                    for t in range(KT):
                        ins = dve.scalar_tensor_tensor(out=tile(at, t), in0=o_ps[:, t, :], scalar=rsum[:, t:t + 1], in1=tile(at, t),
                                                       op0=ALU.mult, op1=ALU.add)
                    ins.then_inc(s_x2, 1)
                if on(n - 1):
                    wait_alone(dve, s_x2, m + 1)
                    for t in range(KT):
                        ins = dve.bn_stats(stats[:, k, t, :], tile(at, t))
                    ins.then_inc(s_st2, 1)
                if on(n - 2):
                    r = n - 2
                    wait_alone(dve, s_rt, r + 1)
                    for t in range(KT):
                        ins = dve.max(top8[:, t, :], rt_ps[:, t * E:(t + 1) * E])
                    ins.then_inc(s_top, 1)
                if on(n - 1):
                    wait_alone(dve, s_st2, m + 1)
                    for t in range(KT):
                        ins = dve.bn_aggr(mv[:, k, t, :], stats[:, k, t, :])
                    ins.then_inc(s_mv, 1)
                if on(n - 2):
                    wait_alone(dve, s_top, r + 1)
                    for t in range(KT):
                        ins = dve.max_index(idx8[:, t, :], top8[:, t, :], rt_ps[:, t * E:(t + 1) * E])
                    ins.then_inc(s_idx, 1)
                if on(n - 2):
                    dve.tensor_copy(xn2r[:, k, :, ID_AT].bitcast(I32), token[:, bass.ds(KT * r, KT)])
                    dve.wait_ge(s_idx, r + 1)
                    dve.tensor_tensor(hot[:], idx8[:, :, 0:TOP_K].unsqueeze(3).to_broadcast([P, KT, TOP_K, E]),
                                      iota_e[:].unsqueeze(1).unsqueeze(1).to_broadcast([P, KT, TOP_K, E]),
                                      ALU.is_equal).then_inc(s_hot, 1)
                with_lo = on(n - 1) and not (isinstance(n, int) and n == B)
                if with_lo:
                    dve.wait_ge(s_hi12, n)
                    lo12(k, e, 0)
                if on(n - 2):
                    dve.wait_ge(s_hot, r + 1)
                    at_least(dve, s_rank, r)
                    dve.tensor_tensor(mask[:], hot[:, :, 0, :], hot[:, :, 1, :], ALU.add).then_inc(s_mask, 1)
                if with_lo:
                    lo12(k, e, 1).then_inc(s_lo12, 1)
                if on(n - 2):
                    dve.wait_ge(s_mask, r + 1)
                    at_least(dve, s_seen, r)
                    dve.tensor_tensor(seen[:, k, 1, :], seen[:, k, 0, :], mask[:, 0, :], ALU.add).then_inc(s_seen1, 1)
                    dve.scalar_tensor_tensor(out=xn2r[:, k, :, W_AT:W_AT + E], in0=rt_ps.rearrange("p (t e) -> p t e", t=KT),
                                             scalar=rt_unscale[:].bitcast(F32), in1=mask[:], op0=ALU.mult, op1=ALU.mult).then_inc(s_rcopy, 1)
                    dve.wait_ge(s_seen1, r + 1)
                    dve.tensor_tensor(seen[:, 1 - k, 0, :], seen[:, k, 1, :], mask[:, 1, :], ALU.add).then_inc(s_seen, 1)
                if with_lo and k == 0:
                    dve.wait_ge(s_hi3, i)
                    lo3(e).then_inc(s_lo3, 1)
            over_batches(dve, step)

            plan = [0]

            def link(ins):
                plan[0] += 1
                ins.then_inc(s_plan, 1)
                dve.wait_ge(s_plan, plan[0])
            dve.wait_ge(s_cnt, 1)
            link(dve.tensor_copy(cnt[:], cnt_ps))
            dve.tensor_tensor(pad_f[:], cnt[0:1, :], region_of[0:1, :], ALU.add)
            link(dve.tensor_scalar(cnt_i[:], cnt[:], float(P - 1), None, ALU.add))
            dve.tensor_copy(pad_i[:], pad_f[:]).then_inc(s_pad_at, 1)
            link(dve.tensor_scalar(ntile[:], cnt_i[:], P.bit_length() - 1, None, ALU.logical_shift_right))
            dve.tensor_scalar(spare[:], ntile[:], -1.0, float(REGION // P), ALU.mult, ALU.add)
            link(dve.tensor_tensor(ntile_upto[:], upto[:], ntile[:].unsqueeze(1).to_broadcast([P, E, E]), ALU.mult))
            link(dve.tensor_reduce(tile_end[:], ntile_upto[:], AX_X, ALU.add))
            link(dve.tensor_tensor(is_past, tile_end[:].unsqueeze(1).to_broadcast([P, MOE_TILES, E]),
                                   iota_i[:].unsqueeze(2).to_broadcast([P, MOE_TILES, E]), ALU.is_le))
            dve.tensor_tensor(past_n[0:1], is_past[0:1], spare[0:1].unsqueeze(1).to_broadcast([1, MOE_TILES, E]), ALU.mult)
            link(dve.tensor_reduce(tile_e, is_past, AX_X, ALU.add))
            dve.tensor_reduce(tile_row[0:1], past_n[0:1], AX_X, ALU.add)
            link(dve.tensor_scalar(tile_e, tile_e, float(E - 1), None, ALU.min))
            dve.tensor_copy(e_i[:], tile_e[0:1])
            link(dve.tensor_tensor(tile_row[0:1], tile_row[0:1], iota_i[0:1], ALU.add))
            dve.tensor_scalar(row_i[:], tile_row[0:1], float(P), pad_f[0:1, E - 1:E], ALU.mult, ALU.min).then_inc(s_map, 1)
            dve.wait_ge(s_tanh, 1)
            unscale(w_unscale[:, 0:2, :], halves[:, 0:2, :], XN_EXP)
            link(unscale(w_unscale[:, 2, :], halves[:, 2, :], 0))
            link(dve.tensor_tensor(unscale_y[:], w_unscale[:, 1, :].bitcast(F32), w_unscale[:, 2, :].bitcast(F32), ALU.mult))
            link(dve.tensor_scalar(unscale_y[:], unscale_y[:], tanh_g[:, 1:2], None, ALU.mult))
            link(dve.tensor_tensor(is_past, tile_e.unsqueeze(2).to_broadcast([P, MOE_TILES, E]),
                                   iota_e[:].unsqueeze(1).to_broadcast([P, MOE_TILES, E]), ALU.is_equal))
            link(dve.tensor_tensor(past_n, is_past, w_unscale[:, 0, :].bitcast(F32).unsqueeze(1).to_broadcast([P, MOE_TILES, E]), ALU.mult))
            dve.tensor_reduce(g_unscale[:], past_n, AX_X, ALU.add).then_inc(s_map, 1)
            link(dve.tensor_tensor(y_unscale[:], is_past, unscale_y[:].unsqueeze(1).to_broadcast([P, MOE_TILES, E]), ALU.mult))

            def take_rows(i, k):
                dve.wait_ge(s_xgt, i + 1)
                dve.tensor_copy(xg_t[:, k], xgt_ps).then_inc(s_xgt_copied, 1)
                dve.tensor_tensor(wsel[:, k], xg[:, k, W_AT:W_AT + E],
                                  y_unscale[:, bass.ds(i, 1), :].rearrange("p a e -> p (a e)"), ALU.mult).then_inc(s_wsel, 1)
                dve.wait_ge(s_wsel, i + 1)
                dve.tensor_reduce(wsum[:, k:k + 1], wsel[:, k], AX_X, ALU.add)

            def moe_step(i, j, k, on):
                if on(i - 1):
                    for h in range(2):
                        dve.wait_ge(s_ht_a, 2 * i - 1 + h)
                        rows, cols = (P, slice(0, KF)) if h == 0 else (HL, slice(KF, KH))
                        dve.tensor_tensor(hid_t[1][0:rows, cols, :], ht_ps[h], hid_t[0][0:rows, cols, :], ALU.subtract).then_inc(s_ht_b, 1)
                if on(i + 1):
                    take_rows(i + 1, 1 - k)
                if on(i):
                    dve.wait_ge(s_silu, i + 1)
                    dve.wait_ge(s_u, i + 1)
                    at_least(dve, s_ht, i)
                    dve.tensor_tensor(hid, u_ps, act_g, ALU.mult).then_inc(s_hmul, 1)
                    if not (isinstance(i, int) and i < 2):
                        dve.wait_ge(s_add[k], 16 * j)
                    dve.tensor_copy(id_s[:, k:k + 1], xg[:, k, ID_AT:ID_AT + 1].bitcast(I32)).then_inc(s_meta, 1)
                    dve.wait_ge(s_hmul, i + 1)
                    dve.tensor_reduce(h_max[:], hid.rearrange("p b h -> p (b h)"), AX_X, ALU.max,
                                      apply_absolute_value=True).then_inc(s_hmax, 1)
                    dve.wait_ge(s_hmax, i + 1)
                    dve.tensor_scalar(h_cap[:], h_max[:], 2.0 ** -100, None, ALU.max).then_inc(s_hcap, 1)
                    dve.wait_ge(s_hcap, i + 1)
                    dve.tensor_scalar(h_exp[:], h_cap[:].bitcast(I32), 255 * ONE, None, ALU.bitwise_and).then_inc(s_hexp, 1)
                    dve.wait_ge(s_hexp, i + 1)
                    dve.tensor_scalar(h_scale[:], h_exp[:], -1.0, 268.0 * ONE, ALU.mult, ALU.add)
                    dve.tensor_scalar(h_unscale[:], h_exp[:], -14.0 * ONE, None, ALU.add).then_inc(s_hscale, 1)
                    dve.wait_ge(s_hscale, i + 1)
                    dve.tensor_scalar(hid, hid, h_scale[:].bitcast(F32), None, ALU.mult).then_inc(s_h, 1)
                    at_least(dve, s_y_copied, i - 1)
                    dve.tensor_scalar(y_scale[:, k:k + 1], wsum[:, k:k + 1], h_unscale[:].bitcast(F32), None, ALU.mult).then_inc(s_yscale, 1)
            over_moe_tiles(dve, moe_step)


def kernel(x, ctx_1024, g_xattn, g_ffn, L0_xattn_wq, L0_xattn_wk, L0_xattn_wv, L0_ffn_Wg, L0_ffn_W1, L0_ffn_W2, L0_ffn_W3):
    import concourse.bacc as bacc
    from concourse.bass_utils import run_bass_kernel_spmd

    e, h, d = L0_ffn_W1.shape
    laid = {
        "x": x,
        "ctxT": np.transpose(ctx_1024, (0, 2, 1)),
        "g_xattn": g_xattn,
        "g_ffn": g_ffn,
        "wqT": np.transpose(L0_xattn_wq),
        "wkT": np.transpose(L0_xattn_wk),
        "wv": L0_xattn_wv,
        "WgT": np.transpose(L0_ffn_Wg),
        "W1T": np.transpose(L0_ffn_W1, (2, 0, 1)).reshape(d, e * h),
        "W2T": np.transpose(L0_ffn_W2, (2, 0, 1)).reshape(d, e * h),
        "W3T": np.transpose(L0_ffn_W3, (2, 0, 1)),
    }
    nc = bacc.Bacc("TRN2", target_bir_lowering=False, num_devices=1, dynamic_dma_scratch_size=8192)
    arrays, args = {}, []
    for name, a in laid.items():
        a = np.ascontiguousarray(a)
        arrays[f"in_{name}"] = a
        args.append(nc.dram_tensor(f"in_{name}", a.shape, mybir.dt.from_np(a.dtype), kind="ExternalInput").ap())
    args.append(nc.dram_tensor("out_0", (x.shape[0] * x.shape[1] + P, x.shape[2]), F32, kind="ExternalOutput").ap())
    gated_cross_attention_and_experts(nc, *args)
    r = run_bass_kernel_spmd(nc, [arrays], core_ids=[0])
    return r.results[0]["out_0"][:x.shape[0] * x.shape[1]].reshape(x.shape)
```
